# Optimizing a Trainium2 kernel written in Bass

```python
import numpy as np
import jax
import jax.numpy as jnp

def _softmax(x, axis=-1):
    return jax.nn.softmax(x, axis=axis)
def _gelu(x):
    return jax.nn.gelu(x, approximate=True)
def _silu(x):
    return jax.nn.silu(x)
def _sigmoid(x):
    return jax.nn.sigmoid(x)
def _layernorm(x, axis=-1, eps=1e-5):
    m = jnp.mean(x, axis=axis, keepdims=True)
    v = jnp.var(x, axis=axis, keepdims=True)
    return (x - m) / jnp.sqrt(v + eps)
def _scatter_add(tgt, idx, src, axis=0):
    return tgt.at[idx].add(src)
def _segment_sum(src, seg, n):
    return jax.ops.segment_sum(src, seg, n)

kernel_name = 'mk_metaformer_d1_conv_nhwc128_d1a0ff'

def setup_inputs(seed: int = 0):
    np.random.seed(seed)
    _w = jnp.asarray
    def _rec_inputs():
        import jax
        import jax.numpy as jnp
        _gk = jax.random.key(seed)
        x = -0.0002091 + 1 * jax.random.normal(jax.random.fold_in(_gk, 1), (16, 112, 112, 128), jnp.float32)
        return x
    x = _rec_inputs()
    def _L0_conv_setup():
        import jax, jax.numpy as jnp
        import numpy as np
        WS = 7
        NH = 8
        C = 128
        HS = C // NH

        def _rel_index(ws):
            coords = np.stack(np.meshgrid(np.arange(ws), np.arange(ws), indexing='ij'), 0).reshape(2, -1)
            rel = coords[:, :, None] - coords[:, None, :] + (ws - 1)
            return jnp.asarray(rel[0] * (2 * ws - 1) + rel[1])
        key = jax.random.key(seed)
        ks = jax.random.split(key, 6)
        B, H, W = (16, 112, 112)
        s = 0.02
        return {'x': jax.random.normal(ks[0], (B, H, W, C), jnp.float32), 'w_q': jax.random.normal(ks[1], (C, C), jnp.float32) * s, 'w_k': jax.random.normal(ks[2], (C, C), jnp.float32) * s, 'w_v': jax.random.normal(ks[3], (C, C), jnp.float32) * s, 'w_o': jax.random.normal(ks[4], (C, C), jnp.float32) * s, 'b_o': jnp.zeros((C,), jnp.float32), 'rel_bias': jax.random.normal(ks[5], ((2 * WS - 1) ** 2, NH), jnp.float32) * s}
    _L0_conv_all = _L0_conv_setup()
    _L0_conv_in = {k: v for k, v in _L0_conv_all.items() if k in ('w_q', 'w_k', 'w_v', 'w_o', 'b_o', 'rel_bias', )}
    del _L0_conv_all

    def _L0_ffn_setup():
        import jax, jax.numpy as jnp
        import numpy as np
        BN_EPS = 1e-05
        key = jax.random.key(seed)
        k1, k2, k3 = jax.random.split(key, 3)
        B, T, I, H = (64, 2048, 128, 128)
        x = jax.random.normal(k1, (B, T, I), dtype=jnp.float32)
        W = jax.random.normal(k2, (H, I), dtype=jnp.float32) * (1.0 / np.sqrt(I))
        V = jnp.linalg.qr(jax.random.normal(k3, (H, H), dtype=jnp.float32))[0]
        gamma = jnp.ones((H,), dtype=jnp.float32)
        beta = jnp.zeros((H,), dtype=jnp.float32)
        return {'x': x, 'W': W, 'V': V, 'gamma': gamma, 'beta': beta}
    _L0_ffn_all = _L0_ffn_setup()
    _L0_ffn_in = {k: v for k, v in _L0_ffn_all.items() if k in ('W', 'V', 'gamma', 'beta', )}
    del _L0_ffn_all

    return {
        "x": x,
        "L0_conv_w_q": _L0_conv_in["w_q"],
        "L0_conv_w_k": _L0_conv_in["w_k"],
        "L0_conv_w_v": _L0_conv_in["w_v"],
        "L0_conv_w_o": _L0_conv_in["w_o"],
        "L0_conv_b_o": _L0_conv_in["b_o"],
        "L0_conv_rel_bias": _L0_conv_in["rel_bias"],
        "L0_ffn_W": _L0_ffn_in["W"],
        "L0_ffn_V": _L0_ffn_in["V"],
        "L0_ffn_gamma": _L0_ffn_in["gamma"],
        "L0_ffn_beta": _L0_ffn_in["beta"],
    }

def reference(x, L0_conv_w_q, L0_conv_w_k, L0_conv_w_v, L0_conv_w_o, L0_conv_b_o, L0_conv_rel_bias, L0_ffn_W, L0_ffn_V, L0_ffn_gamma, L0_ffn_beta):
    import jax
    import jax.numpy as jnp
    def _L0_conv_ref(x, w_q, w_k, w_v, w_o, b_o, rel_bias):
        import jax, jax.numpy as jnp
        import numpy as np
        WS = 7
        NH = 8
        C = 128
        HS = C // NH

        def _rel_index(ws):
            coords = np.stack(np.meshgrid(np.arange(ws), np.arange(ws), indexing='ij'), 0).reshape(2, -1)
            rel = coords[:, :, None] - coords[:, None, :] + (ws - 1)
            return jnp.asarray(rel[0] * (2 * ws - 1) + rel[1])
        B, H, W, Cc = x.shape
        ws = WS
        N = ws * ws
        xw = x.reshape(B, H // ws, ws, W // ws, ws, Cc)
        xw = xw.transpose(0, 1, 3, 2, 4, 5).reshape(-1, N, Cc)
        scale = HS ** (-0.5)
        q = (xw @ w_q).reshape(-1, N, NH, HS).transpose(0, 2, 1, 3) * scale
        k = (xw @ w_k).reshape(-1, N, NH, HS).transpose(0, 2, 1, 3)
        v = (xw @ w_v).reshape(-1, N, NH, HS).transpose(0, 2, 1, 3)
        attn = jnp.einsum('bhnd,bhmd->bhnm', q, k)
        bias = rel_bias[_rel_index(ws)].transpose(2, 0, 1)
        attn = jax.nn.softmax(attn + bias[None], axis=-1)
        o = jnp.einsum('bhnm,bhmd->bhnd', attn, v)
        o = o.transpose(0, 2, 1, 3).reshape(-1, N, Cc)
        o = o @ w_o + b_o
        o = o.reshape(B, H // ws, W // ws, ws, ws, Cc)
        return o.transpose(0, 1, 3, 2, 4, 5).reshape(B, H, W, Cc)

    def _L0_ffn_ref(x, W, V, gamma, beta):
        import jax, jax.numpy as jnp
        import numpy as np
        BN_EPS = 1e-05
        B, T, H = (x.shape[0], x.shape[1], W.shape[0])
        Wx = jnp.einsum('bti,hi->bth', x, W)
        flat = Wx.reshape(B * T, H)
        mean = jnp.mean(flat, axis=0)
        var = jnp.var(flat, axis=0)
        Wx = ((flat - mean) * jax.lax.rsqrt(var + BN_EPS) * gamma + beta).reshape(B, T, H)
        Vt = V.T

        def step(yt, wx_t):
            yt = jax.nn.sigmoid(wx_t + yt @ Vt)
            return (yt, yt)
        y0 = jnp.zeros((B, H), dtype=Wx.dtype)
        _, ys = jax.lax.scan(step, y0, jnp.swapaxes(Wx, 0, 1))
        return jnp.swapaxes(ys, 0, 1)

    def _gn(v, G=32, eps=1e-5):
        B_, H_, W_, C_ = v.shape
        g = v.reshape(B_, H_, W_, G, C_ // G)
        m = jnp.mean(g, axis=(1, 2, 4), keepdims=True)
        s = jnp.var(g, axis=(1, 2, 4), keepdims=True)
        return ((g - m) / jnp.sqrt(s + eps)).reshape(v.shape)

    def _ln_c(v, eps=1e-6):
        m = jnp.mean(v, axis=-1, keepdims=True)
        s = jnp.var(v, axis=-1, keepdims=True)
        return (v - m) / jnp.sqrt(s + eps)

    def _ln_t(v, eps=1e-5):
        m = jnp.mean(v, axis=-1, keepdims=True)
        s = jnp.var(v, axis=-1, keepdims=True)
        return (v - m) / jnp.sqrt(s + eps)

    def _to_tokens(v):
        B_, H_, W_, C_ = v.shape
        return v.reshape(B_, H_ * W_, C_)
    def _from_tokens(t, like):
        return t.reshape(like.shape)

    x = x + _L0_conv_ref(_ln_c(x), L0_conv_w_q, L0_conv_w_k, L0_conv_w_v, L0_conv_w_o, L0_conv_b_o, L0_conv_rel_bias)
    t = _to_tokens(x)
    t = t + _L0_ffn_ref(_ln_t(t), L0_ffn_W, L0_ffn_V, L0_ffn_gamma, L0_ffn_beta)
    x = _from_tokens(t, x)
    return x


_drawn_inputs = setup_inputs


def setup_inputs(seed=0):
    import zlib

    import numpy as np

    out = dict(_drawn_inputs(seed))
    spreads = {'L0_conv_b_o': (0.0, 0.1), 'L0_ffn_gamma': (1.0, 0.556), 'L0_ffn_beta': (0.0, 0.414)}
    factors = {'L0_conv_w_q': 8.0,
     'L0_conv_w_k': 8.0,
     'L0_conv_w_v': 8.0,
     'L0_conv_w_o': 8.0,
     'L0_conv_rel_bias': 8.0}
    for name, (base, spread) in spreads.items():
        noise = np.random.default_rng([zlib.crc32(name.encode()), seed]).standard_normal(out[name].shape)
        drawn = base * np.exp(spread * noise) if base else spread * noise
        out[name] = jnp.asarray(drawn.astype(out[name].dtype))
    for name, factor in factors.items():
        out[name] = (out[name] * factor).astype(out[name].dtype)
    return out
```

```python
from contextlib import ExitStack

import concourse.bass as bass
from concourse import mybir

F32 = mybir.dt.float32
BF16 = mybir.dt.bfloat16
I32 = mybir.dt.int32
ALU = mybir.AluOpType
ACT = mybir.ActivationFunctionType
AX_X = mybir.AxisListType.X

C = 128
NH, HS = 8, 16
WS = 7
N = WS * WS
NW = 16
PW = WS * NW
ST = NW * N
HP = NH // 2
PAIRS = NW // 2
HN = NH * N
REC = C + 2
HALF = ST // 2
CS = 4
NG = 4
WARM = 16
LN1_EPS, LN2_EPS, BN_EPS = 1e-6, 1e-5, 1e-5
SAME = 1e-6

SHARED = [("xT", 0, 1, 0), ("xT", 1, 1, 0), ("k", 0, 1, 1), ("k", 1, 1, 1), ("o", 0, -1, 2), ("o", 1, -1, 2),
          ("v", 0, 1, 3), ("v", 1, 1, 3), ("q", 0, 1, 4), ("q", 1, 1, 5),
          ("x2T", 0, -1, 7), ("x2T", 1, -1, 7), ("w", 0, -1, 8), ("w", 1, -1, 9)]
SLOTS = PAIRS + 3
TILES = [(0, 4), (4, 7)]


def at_strip(dram, strip):
    return dram[bass.ds(strip, 1)].rearrange("s p t c -> (s p) t c")


def at_least(eng, semaphore, value):
    if not (isinstance(value, int) and value <= 0):
        eng.wait_ge(semaphore, value)


def build(nc, images, x, w_q, w_k, w_v, w_o, b_o, rel_bias, ffn_w, ffn_wT, ffn_vT, gamma, beta, ident, sel, x1_rec, out):
    NS = x.shape[0]
    with ExitStack() as ctx:
        def sb(name, shape, dt=F32):
            return ctx.enter_context(nc.sbuf_tensor(name, shape, dt))

        def sem(name):
            return ctx.enter_context(nc.semaphore(name))

        identity = sb("identity", [128, 128])
        ident_b = sb("ident_b", [128, 128], BF16)
        wT_f = sb("wT_f", [128, C])
        minus_half = sb("minus_half", [128, WS])
        w_stats = sb("w_stats", [128, 2 * NS, 6])
        consts = sem("consts")
        made = sem("made")
        phase_a(nc, NS, x, w_q, w_k, w_v, w_o, b_o, rel_bias, ffn_wT, ident, sel, x1_rec,
                identity, ident_b, wT_f, minus_half, w_stats, consts, made)
        phase_b(nc, NS, 2 * NS // images, x1_rec, ffn_w, ffn_vT, gamma, beta, out, identity, minus_half, w_stats)


def phase_a(nc, NS, x, w_q, w_k, w_v, w_o, b_o, rel_bias, ffn_wT, ident, sel, x1_rec,
            identity, ident_b, wT_f, minus_half, w_stats, consts, made):
    with ExitStack() as ctx:
        def sb(name, shape, dt=F32):
            return ctx.enter_context(nc.sbuf_tensor(name, shape, dt))

        def sem(name):
            return ctx.enter_context(nc.semaphore(name))

        wq = sb("wq", [128, C])
        wk = sb("wk", [128, C])
        wv = sb("wv", [128, C])
        wo = sb("wo", [128, C])
        bo = sb("bo", [PW, C])
        sel_f = sb("sel_f", [2 * N, 130])
        sel_b = sb("sel_b", [2 * N, 128], BF16)
        bias_f = sb("bias_f", [2 * N, HN])
        bias_r = sb("bias_r", [2 * N, HN])
        bias_hi = sb("bias_hi", [2 * N, HN], BF16)
        bias_mid = sb("bias_mid", [2 * N, HN], BF16)
        bias_lo = sb("bias_lo", [2 * N, HN], BF16)
        bias_hm = sb("bias_hm", [2 * N, HN], BF16)
        xs = [sb(f"xs{i}", [PW, WS, C]) for i in range(2)]
        xb = [sb(f"xb{i}", [PW, WS, C]) for i in range(2)]
        rec = [sb(f"rec{i}", [PW, WS, REC]) for i in range(2)]
        bn1 = sb("bn1", [PW, WS, 6])
        mv1 = sb("mv1", [PW, WS, 2])
        consts7 = sb("consts7", [PW, 4])
        st_tmp = [sb(f"st_tmp{i}", [PW, 4, WS, 2]) for i in range(2)]
        xn = sb("xn", [PW, WS, C])
        bn2 = sb("bn2", [PW, WS, 6])
        x2n = sb("x2n", [PW, WS, C])
        xT = sb("xT", [C, NW, N])
        kT = sb("kT", [C, NW, N])
        qT = [sb(f"qT{i}", [C, ST + 16]) for i in range(2)]
        kx = [sb(f"kx{i}", [C, NH, ST]) for i in range(2)]
        vv = sb("vv", [2 * N, PAIRS, C])
        v2 = [sb(f"v2{i}", [2 * N, NW, C]) for i in range(2)]
        oT = sb("oT", [C, N, NW])
        x2T = sb("x2T", [C, ST])
        negmax = [sb(f"negmax{i}", [128, NH]) for i in range(2)]
        nm_hi = [sb(f"nm_hi{i}", [128, NH], BF16) for i in range(2)]
        nm_lo = [sb(f"nm_lo{i}", [128, NH], BF16) for i in range(2)]
        den = [sb(f"den{i}", [128, NH]) for i in range(2)]
        rden = [sb(f"rden{i}", [128, NH]) for i in range(2)]
        p = [sb(f"p{i}", [128, HN]) for i in range(2)]
        pT = [sb(f"pT{i}", [2 * N, HP, 2, N]) for i in range(2)]
        bank = [ctx.enter_context(nc.psum_tensor(f"bank{i}", [128, 512], F32)) for i in range(8)]
        s_bank, pT_bank, o_bank, sh_bank = bank[0:2], bank[2:4], bank[4:6], bank[6:8]

        x_in = [sem("x_in0"), sem("x_in1")]
        xn_ready = sem("xn_ready")
        xb_ready = sem("xb_ready")
        psum = {k: sem(f"{k}_psum") for k in ("xT", "k", "v", "q", "o", "x2T", "w")}
        evac = {k: sem(f"{k}_evac") for k in ("xT", "k", "v", "q", "o", "x2T", "w")}
        kx_in = [sem("kx_in0"), sem("kx_in1")]
        v2_in = [sem("v2_in0"), sem("v2_in1")]
        rec_out = [sem("rec_out0"), sem("rec_out1")]
        s_psum = sem("s_psum")
        max_ready = sem("max_ready")
        hi_ready = sem("hi_ready")
        lo_ready = sem("lo_ready")
        shifted = sem("shifted")
        exp_ready = sem("exp_ready")
        sum_ready = sem("sum_ready")
        rden_ready = sem("rden_ready")
        p_ready = sem("p_ready")
        pT_psum = sem("pT_psum")
        pT_evac = sem("pT_evac")
        av_psum = sem("av_psum")
        oT_evac = sem("oT_evac")
        st_steps = [sem("st1_steps"), sem("st2_steps")]
        ve_ready = [sem("ve1_ready"), sem("ve2_ready")]
        bn1_ready = sem("bn1_ready")
        bn2_ready = sem("bn2_ready")
        rs1_ready = sem("rs1_ready")
        rs2_ready = sem("rs2_ready")
        x2n_ready = sem("x2n_ready")
        setup = sem("setup")

        READER = {"xT": "act", "k": "act", "v": "act", "q": "act", "x2T": "act", "o": "dve", "w": "dve"}

        def exists(strip):
            return (not isinstance(strip, int)) or 0 <= strip < NS

        def wait_bank(eng, s, use):
            u, back = use, s
            while True:
                u -= 2
                if u < 0:
                    u += len(SHARED)
                    back = back - 1
                if isinstance(back, int) and back < -1:
                    return
                what, part, rel, _ = SHARED[u]
                if exists(back + rel):
                    eng.wait_ge(evac[what], 2 * (back + rel) + part + 1)
                    return

        def bodies(eng, body):
            for s in (-2, -1, 0, 1):
                body(s // 2, s % 2)
            with eng.Fori(1, NS // 2 - 1) as half:
                body(half, 0)
                body(half, 1)
            for s in (NS - 2, NS - 1, NS):
                body(s // 2, s % 2)

        block = ctx.enter_context(nc.Block())

        @block.sync
        def _(sp):
            for dst, src in ((wq, w_q), (wk, w_k), (wv, w_v), (wo, w_o), (wT_f, ffn_wT), (identity, ident), (sel_f, sel)):
                sp.dma_start(dst[:, :], src).then_inc(consts, 16)
            sp.dma_start(bo[:, :], b_o.partition_broadcast(PW)).then_inc(consts, 16)
            for n in range(N):
                t, r = n // WS, n % WS
                first = (WS - 1 - t) * (2 * WS - 1) + (WS - 1 - r)
                src = bass.AP(rel_bias.tensor, rel_bias.offset + first,
                              [[1, 1], [(2 * WS - 1) ** 2, NH], [2 * WS - 1, WS], [1, WS]])
                sp.dma_start(bias_f[n:n + 1, :].rearrange("p (h t r) -> p h t r", h=NH, t=WS), src,
                             allow_slow_non_contiguous=True).then_inc(consts, 16)
            sp.wait_ge(setup, 11)
            sp.wait_ge(consts, 16 * (NCONST - 1))
            sp.dma_start(bias_f[N:2 * N, :], bias_f[0:N, :]).then_inc(consts, 16)

            def body(half, par):
                s = 2 * half + par
                if exists(s + 2):
                    at_least(sp, xn_ready, s + 1)
                    at_least(sp, xb_ready, s + 1)
                    sp.dma_start(xs[par][:, :, :], at_strip(x, s + 2)).then_inc(x_in[par], 16)
                if exists(s + 1):
                    at_least(sp, evac["k"], 2 * (s + 2))
                    for h in range(NH):
                        sp.dma_start(kx[1 - par][HS * h:HS * h + HS, h, :],
                                     kT[HS * h:HS * h + HS, :, :].rearrange("p a b -> p (a b)")).then_inc(kx_in[1 - par], 16)
                    at_least(sp, evac["v"], 2 * (s + 2))
                    for odd in range(2):
                        for i in range(2):
                            dst = v2[1 - par][odd * N:odd * N + N, :, 64 * odd:64 * odd + 64]
                            sp.dma_start(dst.rearrange("p (q i) c -> p q i c", i=2)[:, :, i, :],
                                         vv[i * N:i * N + N, :, 64 * odd:64 * odd + 64]).then_inc(v2_in[1 - par], 16)
                if exists(s - 1):
                    sp.wait_ge(x2n_ready, s)
                    sp.dma_start(at_strip(x1_rec, s - 1), rec[1 - par][:, :, :]).then_inc(rec_out[1 - par], 16)

            bodies(sp, body)
            for i in range(2):
                sp.wait_ge(rec_out[i], 16 * (NS // 2))

        @block.gpsimd
        def _(pool):
            nc.gpsimd.memset(minus_half[:, :], -0.5).then_inc(setup, 1)
            nc.gpsimd.memset(consts7[:, 0:1], 0.5).then_inc(setup, 1)
            nc.gpsimd.memset(consts7[:, 1:2], 1.0 / C).then_inc(setup, 1)
            nc.gpsimd.memset(consts7[:, 2:3], LN1_EPS).then_inc(setup, 1)
            nc.gpsimd.memset(consts7[:, 3:4], LN2_EPS).then_inc(setup, 1)
            nc.gpsimd.memset(kx[0][:, :, :], 0.0).then_inc(setup, 1)
            nc.gpsimd.memset(kx[1][:, :, :], 0.0).then_inc(setup, 1)
            nc.gpsimd.memset(v2[0][:, :, :], 0.0).then_inc(setup, 1)
            nc.gpsimd.memset(v2[1][:, :, :], 0.0).then_inc(setup, 1)
            nc.gpsimd.memset(qT[0][:, ST:ST + 16], 0.0).then_inc(setup, 1)
            nc.gpsimd.memset(qT[1][:, ST:ST + 16], 0.0).then_inc(setup, 1)
            pool.wait_ge(consts, 16 * NCONST)
            pool.wait_ge(setup, 11)

            def statistics(bn, mean, rstd, eps, which, strip, ready):
                step = st_steps[which]
                t0, t1, t2, t3 = (st_tmp[which][:, k] for k in range(4))
                done = 7 * strip
                pair = bn[:, :, :].rearrange("p t (h k) -> p t h k", h=2)
                TT = nc.gpsimd.tensor_tensor
                half = consts7[:, 0:1, None].to_broadcast([PW, WS, 2])
                per = consts7[:, 1:2, None].to_broadcast([PW, WS, 2])
                at_least(pool, step, done)
                TT(t0, pair[:, :, :, 1], half, ALU.mult).then_inc(step, 1)
                TT(t1, pair[:, :, :, 2], per, ALU.mult).then_inc(step, 1)
                pool.wait_ge(step, done + 2)
                TT(mean, t0[:, :, 0], t0[:, :, 1], ALU.add).then_inc(step, 1)
                TT(t2[:, :, 0], t0[:, :, 0], t0[:, :, 1], ALU.subtract).then_inc(step, 1)
                TT(t3[:, :, 0], t1[:, :, 0], t1[:, :, 1], ALU.add).then_inc(step, 1)
                pool.wait_ge(step, done + 4)
                TT(t2[:, :, 1], t2[:, :, 0], t2[:, :, 0], ALU.mult).then_inc(step, 1)
                pool.wait_ge(step, done + 6)
                TT(t3[:, :, 1], t3[:, :, 0], t2[:, :, 1], ALU.add).then_inc(step, 1)
                pool.wait_ge(step, done + 7)
                TT(t1[:, :, 0], t3[:, :, 1], consts7[:, 2 + which:3 + which].to_broadcast([PW, WS]), ALU.add)\
                    .then_inc(ve_ready[which], 1)
                pool.wait_ge(ve_ready[which], strip + 1)
                TT(rstd, t1[:, :, 0], minus_half[0:PW, :], ALU.pow).then_inc(ready, 1)

            def body(half, par):
                s = 2 * half + par
                for slot in range(SLOTS):
                    if slot == 3 and exists(s + 1):
                        pool.wait_ge(x_in[1 - par], 16 * nth(half, par, 1))
                        at_least(pool, evac["o"], 2 * s)
                        nc.gpsimd.tensor_tensor(xb[1 - par][:, :, :], xs[1 - par][:, :, :],
                                                bo[:, None, :].to_broadcast([PW, WS, C]), ALU.add).then_inc(xb_ready, 1)
                    g = slot - 1
                    if 0 <= g < PAIRS and exists(s):
                        pool.wait_ge(rden_ready, PAIRS * s + g + 1)
                        pv = p[g % 2][:, :].rearrange("p (h m) -> p h m", h=NH)
                        nc.gpsimd.tensor_tensor(pv, pv, rden[g % 2][:, :, None].to_broadcast([128, NH, N]),
                                                ALU.mult).then_inc(p_ready, 1)

                    if slot == 4 and exists(s - 1):
                        pool.wait_ge(bn2_ready, s)
                        statistics(bn2, rec[1 - par][:, :, C], rec[1 - par][:, :, C + 1], LN2_EPS, 1, s - 1, rs2_ready)
                    if slot == 7 and exists(s + 2):
                        pool.wait_ge(bn1_ready, s + 3)
                        at_least(pool, xn_ready, s + 2)
                        statistics(bn1, mv1[:, :, 0], mv1[:, :, 1], LN1_EPS, 0, s + 2, rs1_ready)

            bodies(pool, body)

        @block.tensor
        def _(pe):
            pe.wait_ge(consts, 16 * NCONST)
            pe.wait_ge(setup, 11)
            pe.wait_ge(made, 8)

            def shared(s, par, use):
                what, part, rel, _ = SHARED[use]
                if not exists(s + rel):
                    return
                strip = s + rel
                dst = sh_bank[use % 2]
                lo, hi = TILES[part]
                wait_bank(pe, s, use)
                if what == "xT":
                    if part == 0:
                        pe.wait_ge(xn_ready, strip + 1)
                    for t in range(lo, hi):
                        mm = nc.tensor.transpose(dst[:, (t - lo) * PW:(t - lo + 1) * PW], xn[:, t, :],
                                                 identity[0:PW, 0:PW])
                elif what in ("q", "k"):
                    if what == "k":
                        pe.wait_ge(evac["xT"], 2 * (strip + 1))
                    w = wq if what == "q" else wk
                    mm = nc.tensor.matmul(dst[:, 0:ST // 2], w[:, :],
                                          xT[:, part * NW // 2:(part + 1) * NW // 2, :], start=True, stop=True)
                elif what == "v":
                    for i in range(4):
                        pr = 4 * part + i
                        mm = nc.tensor.matmul(dst[0:2 * N, i * C:(i + 1) * C], xT[:, 2 * pr:2 * pr + 2, :], wv[:, :],
                                              start=True, stop=True)
                elif what == "o":
                    pe.wait_ge(oT_evac, 2 * (strip + 1))
                    for t in range(lo, hi):
                        mm = nc.tensor.matmul(dst[0:PW, (t - lo) * C:(t - lo + 1) * C],
                                              oT[:, t * WS:(t + 1) * WS, :], wo[:, :], start=True, stop=True)
                elif what == "x2T":
                    if part == 0:
                        pe.wait_ge(x2n_ready, strip + 1)
                    for t in range(lo, hi):
                        mm = nc.tensor.transpose(dst[:, (t - lo) * PW:(t - lo + 1) * PW], x2n[:, t, :],
                                                 identity[0:PW, 0:PW])
                else:
                    if part == 0:
                        pe.wait_ge(evac["x2T"], 2 * (strip + 1))
                    mm = nc.tensor.matmul(dst[:, 0:ST // 2], wT_f[:, :], x2T[:, part * (ST // 2):(part + 1) * (ST // 2)],
                                          start=True, stop=True)
                mm.then_inc(psum[what], 1)

            def body(half, par):
                s = 2 * half + par
                for slot in range(SLOTS):
                    g = slot
                    if g < PAIRS and exists(s):
                        if g == 0:
                            pe.wait_ge(evac["q"], 2 * (s + 1))
                            pe.wait_ge(kx_in[par], 16 * NH * nth(half, par))
                        at_least(pe, exp_ready, PAIRS * s + g - 1)
                        sb_ = s_bank[g % 2][:, 0:HN]
                        nc.tensor.matmul(sb_, sel_b[:, :], bias_hm[:, :], start=True, stop=False,
                                         skip_group_check=True)
                        nc.tensor.matmul(sb_, sel_b[0:N, :], bias_lo[0:N, :], start=False, stop=False,
                                         skip_group_check=True)
                        for i in range(2):
                            w = 2 * g + i
                            mm = nc.tensor.matmul(s_bank[g % 2][64 * i:64 * i + 64, 0:HN], qT[par][:, N * w:N * w + 64],
                                                  kx[par][:, :, N * w:N * w + N], start=False, stop=(i == 1),
                                                  skip_group_check=True)
                        mm.then_inc(s_psum, 1)
                    g = slot - 1
                    if 0 <= g < PAIRS and exists(s):
                        pe.wait_ge(lo_ready, PAIRS * s + g + 1)
                        sb_ = s_bank[g % 2][:, 0:HN]
                        for k, part in enumerate((nm_hi, nm_lo)):
                            mm = nc.tensor.matmul(sb_, ident_b[:, :], part[g % 2][:, :, None].to_broadcast([128, NH, N]),
                                                  start=False, stop=(k == 1), skip_group_check=True)
                        mm.then_inc(shifted, 1)
                    for use in range(len(SHARED)):
                        if SHARED[use][3] == slot:
                            shared(s, par, use)
                    g = slot - 2
                    if 0 <= g < PAIRS and exists(s):
                        pe.wait_ge(p_ready, PAIRS * s + g + 1)
                        at_least(pe, pT_evac, PAIRS * s + g - 1)
                        for j in range(HP):
                            mm = nc.tensor.transpose(pT_bank[g % 2][0:2 * N, 128 * j:128 * j + 128],
                                                     p[g % 2][:, 2 * N * j:2 * N * (j + 1)], identity[:, :])
                        mm.then_inc(pT_psum, 1)
                    g = slot - 3
                    if 0 <= g < PAIRS and exists(s):
                        if g == 0:
                            pe.wait_ge(v2_in[par], 16 * 4 * nth(half, par))
                        pe.wait_ge(pT_evac, PAIRS * s + g + 1)
                        if g % 4 == 0:
                            at_least(pe, oT_evac, 2 * s + g // 4 - 1)
                        for i in range(2):
                            col = (2 * (g % 4) + i) * N
                            for j in range(HP):
                                lhs = v2[par][:, 2 * g + i, j:C:HP]
                                mm = nc.tensor.matmul(o_bank[g // 4][32 * j:32 * j + 32, col:col + N], lhs,
                                                      pT[g % 2][:, j, i, :], start=True, stop=True,
                                                      tile_position=(0, 32 * j))
                        mm.then_inc(av_psum, 1)

            bodies(pe, body)

        @block.scalar
        def _(act):
            def read_shared(half, par, use):
                s = 2 * half + par
                what, part, rel, _ = SHARED[use]
                if READER[what] != "act" or not exists(s + rel):
                    return
                strip = s + rel
                src = sh_bank[use % 2]
                lo, hi = TILES[part]
                act.wait_ge(psum[what], 2 * strip + part + 1)
                if what == "xT":
                    if part == 0:
                        at_least(act, psum["q"], 2 * strip)
                    nn = (hi - lo) * WS
                    ins = nc.scalar.activation(xT[:, :, lo * WS:hi * WS],
                                               src[:, 0:nn * NW].rearrange("p (n w) -> p w n", w=NW), ACT.Copy)
                elif what == "k":
                    if part == 0:
                        wait_spread(half, par, strip)
                    ins = nc.scalar.activation(kT[:, part * NW // 2:(part + 1) * NW // 2, :],
                                               src[:, 0:ST // 2].rearrange("p (w n) -> p w n", n=N), ACT.Copy)
                elif what == "q":
                    if part == 0:
                        at_least(act, s_psum, PAIRS * (strip - 1))
                    ins = nc.scalar.activation(qT[1 - par][:, part * (ST // 2):(part + 1) * (ST // 2)],
                                               src[:, 0:ST // 2], ACT.Copy, scale=float(HS) ** -0.5)
                elif what == "v":
                    if part == 0:
                        wait_v2(half, par, strip)
                    ins = nc.scalar.activation(vv[:, 4 * part:4 * part + 4, :],
                                               src[0:2 * N, :].rearrange("p (q c) -> p q c", c=C), ACT.Copy)
                else:
                    if part == 0:
                        at_least(act, psum["w"], 2 * strip)
                    ins = nc.scalar.activation(x2T[:, lo * PW:hi * PW], src[:, 0:(hi - lo) * PW], ACT.Copy)
                ins.then_inc(evac[what], 1)

            def wait_spread(half, par, strip):
                if exists(strip - 1):
                    act.wait_ge(kx_in[par], 16 * NH * nth(half, par))

            def wait_v2(half, par, strip):
                if exists(strip - 1):
                    act.wait_ge(v2_in[par], 16 * 4 * nth(half, par))

            def body(half, par):
                s = 2 * half + par
                for slot in range(SLOTS):
                    g = slot - 1
                    if 0 <= g < PAIRS and exists(s):
                        act.wait_ge(shifted, PAIRS * s + g + 1)
                        at_least(act, pT_psum, PAIRS * s + g - 1)
                        nc.scalar.activation(p[g % 2][:, :], s_bank[g % 2][:, 0:HN], ACT.Exp).then_inc(exp_ready, 1)
                    for use in range(len(SHARED)):
                        if SHARED[use][3] == slot:
                            read_shared(half, par, use)
                    g = slot - 2
                    if 0 <= g < PAIRS and exists(s):
                        act.wait_ge(pT_psum, PAIRS * s + g + 1)
                        at_least(act, av_psum, PAIRS * s + g - 1)
                        src = pT_bank[g % 2][0:2 * N, :].rearrange("p (j i n) -> p j i n", j=HP, i=2)[:, :, :, 0:N]
                        nc.scalar.activation(pT[g % 2][:, :, :, :], src, ACT.Copy).then_inc(pT_evac, 1)
                    g = slot - 3
                    if 0 <= g < PAIRS and g % 4 == 3 and exists(s):
                        act.wait_ge(av_psum, PAIRS * s + g + 1)
                        at_least(act, psum["o"], 2 * s)
                        b = g // 4
                        nc.scalar.activation(oT[:, :, 8 * b:8 * b + 8],
                                             o_bank[b][:, 0:8 * N].rearrange("p (w n) -> p n w", n=N),
                                             ACT.Copy).then_inc(oT_evac, 1)

            bodies(act, body)

        @block.vector
        def _(dve):
            dve.wait_ge(consts, 16 * NCONST)
            nc.vector.tensor_copy(ident_b[:, :], identity[:, :]).then_inc(made, 1)
            nc.vector.tensor_copy(sel_b[:, :], sel_f[:, 0:128]).then_inc(made, 1)
            nc.vector.tensor_copy(bias_hi[:, :], bias_f[:, :]).then_inc(made, 1)
            dve.wait_ge(made, 3)
            nc.vector.tensor_tensor(bias_r[:, :], bias_f[:, :], bias_hi[:, :], ALU.subtract).then_inc(made, 1)
            dve.wait_ge(made, 4)
            nc.vector.tensor_copy(bias_mid[:, :], bias_r[:, :]).then_inc(made, 1)
            dve.wait_ge(made, 5)
            nc.vector.tensor_tensor(bias_lo[:, :], bias_r[:, :], bias_mid[:, :], ALU.subtract).then_inc(made, 1)
            dve.wait_ge(made, 6)
            nc.vector.tensor_scalar(bias_r[:, :], bias_mid[:, :], sel_f[:, 129:130], None, ALU.mult).then_inc(made, 1)
            dve.wait_ge(made, 7)
            nc.vector.scalar_tensor_tensor(bias_hm[:, :], bias_hi[:, :], sel_f[:, 128:129], bias_r[:, :],
                                           ALU.mult, ALU.add).then_inc(made, 1)

            def ln1(half, par, step):
                s = 2 * half + par
                if not exists(s + 2):
                    return
                if step == 0:
                    dve.wait_ge(x_in[par], 16 * nth(half, par, 2))
                    at_least(dve, rs1_ready, s + 2)
                    for t in range(WS):
                        ins = nc.vector.bn_stats(bn1[:, t, :], xs[par][:, t, :])
                    ins.then_inc(bn1_ready, 1)
                else:
                    dve.wait_ge(rs1_ready, s + 3)
                    at_least(dve, psum["xT"], 2 * (s + 2))
                    for t in range(WS):
                        ins = nc.vector.tensor_scalar(xn[:, t, :], xs[par][:, t, :], mv1[:, t, 0:1], mv1[:, t, 1:2],
                                                      ALU.subtract, ALU.mult)
                    ins.then_inc(xn_ready, 1)

            def ln2(s, par, step):
                if not exists(s - 1):
                    return
                r = rec[1 - par]
                if step == 0:
                    at_least(dve, rs2_ready, s - 1)
                    dve.wait_ge(evac["o"], 2 * s)
                    for t in range(WS):
                        ins = nc.vector.bn_stats(bn2[:, t, :], r[:, t, 0:C])
                    ins.then_inc(bn2_ready, 1)
                else:
                    dve.wait_ge(rs2_ready, s)
                    at_least(dve, psum["x2T"], 2 * (s - 1))
                    for t in range(WS):
                        ins = nc.vector.tensor_scalar(x2n[:, t, :], r[:, t, 0:C], r[:, t, C:C + 1],
                                                      r[:, t, C + 1:C + 2], ALU.subtract, ALU.mult)
                    ins.then_inc(x2n_ready, 1)

            def read_shared(half, par, use):
                s = 2 * half + par
                what, part, rel, _ = SHARED[use]
                if READER[what] != "dve" or not exists(s + rel):
                    return
                strip = s + rel
                src = sh_bank[use % 2]
                lo, hi = TILES[part]
                dve.wait_ge(psum[what], 2 * strip + part + 1)
                if what == "o":
                    if part == 0:
                        dve.wait_ge(xb_ready, strip + 1)
                        if not (isinstance(strip, int) and strip < 2):
                            dve.wait_ge(rec_out[1 - par], 16 * nth(half, par, -3))
                    nc.vector.tensor_tensor(rec[1 - par][:, lo:hi, 0:C],
                                            src[0:PW, 0:(hi - lo) * C].rearrange("p (t c) -> p t c", c=C),
                                            xb[1 - par][:, lo:hi, :], ALU.add).then_inc(evac["o"], 1)
                else:
                    nc.vector.bn_stats(w_slot(strip, part), src[:, 0:ST // 2]).then_inc(evac["w"], 1)

            def w_slot(strip, part):
                return w_stats[:, bass.ds(2 * strip + part, 1), :]

            def body(half, par):
                s = 2 * half + par
                for slot in range(SLOTS):
                    g = slot
                    if g < PAIRS and exists(s):
                        dve.wait_ge(s_psum, PAIRS * s + g + 1)
                        at_least(dve, lo_ready, PAIRS * s + g - 1)
                        nc.vector.tensor_reduce(negmax[g % 2][:, :], s_bank[g % 2][:, 0:HN].rearrange("p (h m) -> p h m", h=NH),
                                                AX_X, ALU.max, negate=True).then_inc(max_ready, 1)
                    if 1 <= slot <= PAIRS and exists(s):
                        dve.wait_ge(exp_ready, PAIRS * s + g)
                        at_least(dve, rden_ready, PAIRS * s + g - 2)
                        nc.vector.tensor_reduce(den[(g - 1) % 2][:, :], p[(g - 1) % 2][:, :].rearrange("p (h m) -> p h m", h=NH),
                                                AX_X, ALU.add).then_inc(sum_ready, 1)
                    if g < PAIRS and exists(s):
                        dve.wait_ge(max_ready, PAIRS * s + g + 1)
                        at_least(dve, shifted, PAIRS * s + g - 1)
                        nc.vector.tensor_copy(nm_hi[g % 2][:, :], negmax[g % 2][:, :]).then_inc(hi_ready, 1)
                    if 1 <= slot <= PAIRS and exists(s):
                        dve.wait_ge(sum_ready, PAIRS * s + g)
                        at_least(dve, p_ready, PAIRS * s + g - 2)
                        nc.vector.reciprocal(rden[(g - 1) % 2][:, :], den[(g - 1) % 2][:, :]).then_inc(rden_ready, 1)
                    if g < PAIRS and exists(s):
                        dve.wait_ge(hi_ready, PAIRS * s + g + 1)
                        nc.vector.tensor_tensor(nm_lo[g % 2][:, :], negmax[g % 2][:, :], nm_hi[g % 2][:, :],
                                                ALU.subtract).then_inc(lo_ready, 1)
                    for use in range(len(SHARED)):
                        if SHARED[use][3] == slot:
                            read_shared(half, par, use)
                    if slot in (3, 5):
                        ln2(s, par, slot - 3)
                    if slot in (6, 8):
                        ln1(half, par, slot - 6)

            bodies(dve, body)


NCONST = 8 + N + 1


def nth(half, par, ahead=0):
    return half + (par + ahead) // 2 + 1


def phase_b(nc, NS, SEGS, x1_rec, ffn_w, ffn_vT, gamma, beta, out, identity, minus_half, w_stats):
    NG = 2 * NS // 128
    COLS = 128 * NG
    CHUNKS = HALF // CS
    WCH = WARM // CS
    recs = x1_rec.rearrange("s p t c -> (s p t) c").rearrange("(g p u) c -> p g u c", g=NG, u=HALF)
    outs = out.rearrange("(g p u) c -> p g u c", g=NG, u=HALF)
    with ExitStack() as ctx:
        def sb(name, shape, dt=F32):
            return ctx.enter_context(nc.sbuf_tensor(name, shape, dt))

        def sem(name):
            return ctx.enter_context(nc.semaphore(name))

        w = sb("w", [C, C])
        vT = sb("vT", [C, C])
        g_col = sb("g_col", [C, 1])
        b_col = sb("b_col", [C, 1])
        w_mv = sb("w_mv", [C, 2])
        w_ve = sb("w_ve", [C, 1])
        w_rs = sb("w_rs", [C, 1])
        a_col = sb("a_col", [C, 1])
        ma_col = sb("ma_col", [C, 1])
        c_col = sb("c_col", [C, 1])
        w_a = sb("w_a", [C, C])
        w_aT = sb("w_aT", [C, C])
        xr = [sb(f"xr{i}", [128, NG, CS, REC]) for i in range(4)]
        xm = sb("xm", [128, NG, CS, C])
        xmT = [sb(f"xmT{i}", [C, NG, CS * 128]) for i in range(2)]
        y = sb("y", [C, 2 * CS, COLS])
        yo = [sb(f"yo{i}", [128, NG, CS, C]) for i in range(2)]
        ends = sb("ends", [C, COLS])
        diff = sb("diff", [C, COLS])
        dmax = sb("dmax", [C, 1])
        dmax1 = sb("dmax1", [1, 1])
        again_f = sb("again_f", [1, 1])
        again = sb("again", [1, 1], I32)
        bank = [ctx.enter_context(nc.psum_tensor(f"bbank{i}", [128, 512], F32)) for i in range(8)]
        z_bank, xT_bank, yT_bank = bank[0:4], bank[4:6], bank[6:8]

        par_in = sem("par_in")
        prep = sem("prep")
        w_ve_ready = sem("w_ve_ready")
        prep_psum = sem("prep_psum")
        x_in = [sem(f"bx_in{i}") for i in range(4)]
        norm_ready = sem("norm_ready")
        xT_psum = sem("bxT_psum")
        xT_ready = sem("bxT_ready")
        z_psum = sem("z_psum")
        y_ready = sem("y_ready")
        yT_psum = sem("yT_psum")
        yo_ready = sem("yo_ready")
        out_done = [sem("out_done0"), sem("out_done1")]
        start_ready = sem("start_ready")
        dmax_ready = sem("dmax_ready")
        dmax_psum = sem("dmax_psum")
        again_ready = sem("again_ready")
        pass_written = sem("pass_written")
        pass_ended = sem("pass_ended")
        checks = sem("checks")

        class Pass:
            def __init__(self, p):
                self.warm = p is None
                self.p = p
                self.n = WCH if self.warm else CHUNKS
                self.offset = CHUNKS - WCH if self.warm else 0
                self.base = 0 if self.warm else WCH + CHUNKS * p
                self.tail_base = 0 if self.warm else CHUNKS * p

            def loads(self, b, q):
                if self.warm:
                    return 1
                return self.p * ((CHUNKS - b + 3) // 4) + 2 + whole(q, b, 4)

            def stores(self, par, q):
                return self.p * (CHUNKS // 2) + 1 + whole(q, par, 2)

        def whole(q, rest, by):
            return (q - rest) // by if isinstance(q, int) else q4[0] * (4 // by) + (q4[1] + q[1] - rest) // by

        q4 = [None, 0]

        def bodies(eng, ps, body):
            first, last = 4, 4 * ((ps.n - 3) // 4)
            if ps.warm or last - first < 8:
                for q in range(-1, ps.n + 1):
                    body(ps, q, q % 4)
                return
            for q in range(-1, first):
                body(ps, q, q % 4)
            with eng.Fori(first // 4, last // 4) as i:
                for k in range(4):
                    q4[:] = [i, k]
                    body(ps, 4 * i + k, k)
            for q in range(last, ps.n + 1):
                body(ps, q, q % 4)

        def passes(eng, one_pass):
            one_pass(Pass(None))
            one_pass(Pass(0))
            eng.wait_ge(again_ready, 1)
            todo = eng.value_load(again[0:1, 0:1], min_val=0, max_val=1)
            with eng.If(todo != 0):
                with eng.Fori(1, SEGS) as p:
                    still = eng.value_load(again[0:1, 0:1], min_val=0, max_val=1)
                    with eng.If(still != 0):
                        one_pass(Pass(p))
                        eng.wait_ge(again_ready, p + 1)
                        eng.sem_inc(pass_ended, 1)

        def has(ps, q):
            return (not isinstance(q, int)) or 0 <= q < ps.n

        block = ctx.enter_context(nc.Block())

        @block.sync
        def _(sp):
            for dst, src in ((w, ffn_w), (vT, ffn_vT), (g_col, gamma), (b_col, beta)):
                sp.dma_start(dst[:, :], src).then_inc(par_in, 16)

            def body(ps, q, k4):
                if has(ps, q + 2) or (isinstance(q, int) and q == -1):
                    for d in ((1, 2) if isinstance(q, int) and q == -1 else (2,)):
                        b = (k4 + d) % 4
                        behind = 3 if not (isinstance(q, int) and q + d < 4) else q + d
                        if ps.warm or (isinstance(ps.p, int) and isinstance(q, int) and q + d < 4):
                            at_least(sp, norm_ready, NG * (ps.base + q + d - behind))
                        else:
                            sp.wait_ge(yo_ready, NG * (ps.tail_base + q + d - behind))
                        sp.dma_start(xr[b][:, :, :, :],
                                     recs[:, :, bass.ds(CS * (ps.offset + q + d), CS), :]).then_inc(x_in[b], 16)
                if has(ps, q - 1) and not ps.warm:
                    par = (k4 - 1) % 2
                    sp.wait_ge(yo_ready, NG * (ps.tail_base + q))
                    sp.dma_start(outs[:, :, bass.ds(CS * (q - 1), CS), :], yo[par][:, :, :, :]).then_inc(out_done[par], 16)

            def one_pass(ps):
                bodies(sp, ps, body)
                if not ps.warm:
                    for par in range(2):
                        sp.wait_ge(out_done[par], 16 * (ps.p + 1) * (CHUNKS // 2))
                        sp.sem_inc(pass_written, 1)

            passes(sp, one_pass)

        @block.tensor
        def _(pe):
            pe.wait_ge(prep, 6)
            nc.tensor.transpose(xT_bank[0][:, 0:C], w_a[:, :], identity[:, :]).then_inc(prep_psum, 1)
            pe.wait_ge(prep, 7)

            def body(ps, q, k4):
                par = k4 % 2
                for k in range(CS):
                    for g in range(NG):
                        if has(ps, q):
                            cols = slice(128 * g, 128 * g + 128)
                            idx = (CS * (ps.base + q) + k) * NG + g
                            if k == 0:
                                pe.wait_ge(xT_ready, NG * (ps.base + q) + g + 1)
                            if isinstance(q, int) and q == 0 and k == 0 and g == 0:
                                pe.wait_ge(start_ready, 1 if ps.warm else ps.p + 2)
                            at_least(pe, y_ready, idx - NG + 1)
                            nc.tensor.matmul(z_bank[g][:, 0:128], w_aT[:, :], xmT[par][:, g, 128 * k:128 * k + 128],
                                             start=True, stop=False)
                            nc.tensor.matmul(z_bank[g][:, 0:128], vT[:, :], y[:, (par * CS + k - 1) % (2 * CS), cols],
                                             start=False, stop=True).then_inc(z_psum, 1)
                    if k < NG and has(ps, q - 1) and not ps.warm:
                        idx = NG * (ps.tail_base + q - 1) + k
                        use = (NG * (k4 - 1) + k) % 2
                        at_least(pe, yo_ready, idx - 1)
                        at_least(pe, y_ready, CS * NG * (ps.base + q))
                        for i in range(CS):
                            mm = nc.tensor.transpose(yT_bank[use][:, 128 * i:128 * i + 128],
                                                     y[:, (1 - par) * CS + i, 128 * k:128 * k + 128], identity[:, :])
                        mm.then_inc(yT_psum, 1)
                    if k < NG and has(ps, q + 1):
                        idx = NG * (ps.base + q + 1) + k
                        use = (NG * (k4 + 1) + k) % 2
                        pe.wait_ge(norm_ready, idx + 1)
                        at_least(pe, xT_ready, idx - 1)
                        for i in range(CS):
                            mm = nc.tensor.transpose(xT_bank[use][:, 128 * i:128 * i + 128], xm[:, k, i, :],
                                                     identity[:, :])
                        mm.then_inc(xT_psum, 1)

            def one_pass(ps):
                bodies(pe, ps, body)
                if not ps.warm:
                    pe.wait_ge(dmax_ready, ps.p + 1)
                    nc.tensor.transpose(xT_bank[0][0:1, 0:128], dmax[:, :], identity[:, :]).then_inc(dmax_psum, 1)

            passes(pe, one_pass)

        @block.scalar
        def _(act):
            def body(ps, q, k4):
                par = k4 % 2
                if not has(ps, q):
                    return
                for k in range(CS):
                    for g in range(NG):
                        idx = (CS * (ps.base + q) + k) * NG + g
                        act.wait_ge(z_psum, idx + 1)
                        nc.scalar.activation(y[:, par * CS + k, 128 * g:128 * g + 128], z_bank[g][:, 0:128],
                                             ACT.Sigmoid, bias=c_col[:, :]).then_inc(y_ready, 1)

            def one_pass(ps):
                if not ps.warm or True:
                    bodies(act, ps, body)

            act.wait_ge(prep, 6)
            passes(act, one_pass)

        @block.gpsimd
        def _(pool):
            pool.wait_ge(prep, 1)
            nc.gpsimd.tensor_scalar(w_ve[:, :], w_mv[:, 1:2], BN_EPS, None, ALU.add).then_inc(w_ve_ready, 1)
            pool.wait_ge(w_ve_ready, 1)
            nc.gpsimd.tensor_tensor(w_rs[:, :], w_ve[:, :], minus_half[:, 0:1], ALU.pow).then_inc(prep, 1)

        @block.vector
        def _(dve):
            nc.vector.bn_aggr(w_mv[:, :], w_stats[:, :, :].rearrange("p a b -> p (a b)")).then_inc(prep, 1)
            nc.vector.memset(y[:, 2 * CS - 1, :], 0.0).then_inc(start_ready, 1)
            dve.wait_ge(prep, 1)
            dve.wait_ge(prep, 2)
            dve.wait_ge(par_in, 16 * 4)
            nc.vector.tensor_tensor(a_col[:, :], w_rs[:, :], g_col[:, :], ALU.mult).then_inc(prep, 1)
            dve.wait_ge(prep, 3)
            nc.vector.tensor_tensor(ma_col[:, :], w_mv[:, 0:1], a_col[:, :], ALU.mult).then_inc(prep, 1)
            dve.wait_ge(prep, 4)
            nc.vector.tensor_tensor(c_col[:, :], b_col[:, :], ma_col[:, :], ALU.subtract).then_inc(prep, 1)
            nc.vector.tensor_scalar(w_a[:, :], w[:, :], a_col[:, :], None, ALU.mult).then_inc(prep, 1)
            dve.wait_ge(prep_psum, 1)
            nc.vector.tensor_copy(w_aT[:, :], xT_bank[0][:, 0:C]).then_inc(prep, 1)
            dve.wait_ge(prep, 7)

            def body(ps, q, k4):
                par = k4 % 2
                for k in range(min(CS, NG)):
                    if has(ps, q + 1):
                        b = (k4 + 1) % 4
                        idx = NG * (ps.base + q + 1) + k
                        if k == 0:
                            dve.wait_ge(x_in[b], 16 * ps.loads(b, q + 1 if isinstance(q, int) else after(1)))
                        at_least(dve, xT_psum, idx + 1 - NG)
                        for i in range(CS):
                            ins = nc.vector.tensor_scalar(xm[:, k, i, :], xr[b][:, k, i, 0:C], xr[b][:, k, i, C:C + 1],
                                                          xr[b][:, k, i, C + 1:C + 2], ALU.subtract, ALU.mult)
                        ins.then_inc(norm_ready, 1)
                    if has(ps, q - 1) and not ps.warm:
                        b, op = (k4 - 1) % 4, (k4 - 1) % 2
                        idx = NG * (ps.tail_base + q - 1) + k
                        use = (NG * (k4 - 1) + k) % 2
                        dve.wait_ge(yT_psum, idx + 1)
                        if k == 0 and not (isinstance(q, int) and q < 3 and isinstance(ps.p, int) and ps.p == 0):
                            stores = ps.stores(op, q - 1 if isinstance(q, int) else after(-1)) - 1
                            dve.wait_ge(out_done[op], 16 * stores)
                        nc.vector.tensor_tensor(yo[op][:, k, :, :],
                                                yT_bank[use][:, :].rearrange("p (i c) -> p i c", c=C),
                                                xr[b][:, k, :, 0:C], ALU.add).then_inc(yo_ready, 1)
                    if has(ps, q + 1):
                        idx = NG * (ps.base + q + 1) + k
                        use = (NG * (k4 + 1) + k) % 2
                        dve.wait_ge(xT_psum, idx + 1)
                        at_least(dve, z_psum, CS * NG * (ps.base + q))
                        nc.vector.tensor_copy(xmT[1 - par][:, k, :], xT_bank[use][:, :]).then_inc(xT_ready, 1)

            def after(d):
                return ("after", d)

            steps = [0]

            def one_pass(ps):
                bodies(dve, ps, body)
                last = y[:, 2 * CS - 1, :]
                dve.wait_ge(y_ready, CS * NG * (ps.base + ps.n))
                dve.wait_ge(z_psum, CS * NG * (ps.base + ps.n))
                if ps.warm:
                    done = 0
                else:
                    done = 2 + 5 * ps.p
                    nc.vector.tensor_tensor(diff[:, :], last, ends[:, :], ALU.subtract).then_inc(checks, 1)
                    dve.wait_ge(checks, done + 1)
                    nc.vector.tensor_reduce(dmax[:, :], diff[:, :], AX_X, ALU.max, apply_absolute_value=True)\
                        .then_inc(dmax_ready, 1)
                    dve.wait_ge(dmax_psum, ps.p + 1)
                    nc.vector.tensor_reduce(dmax1[:, :], xT_bank[0][0:1, 0:128], AX_X, ALU.max).then_inc(checks, 1)
                    dve.wait_ge(checks, done + 2)
                    nc.vector.tensor_scalar(again_f[:, :], dmax1[:, :], SAME, None, ALU.is_gt).then_inc(checks, 1)
                    dve.wait_ge(checks, done + 3)
                    done = done + 3
                nc.vector.tensor_copy(ends[:, :], last).then_inc(checks, 1)
                dve.wait_ge(checks, done + 1)
                nc.vector.tensor_copy(y[:, 2 * CS - 1, 1:COLS], ends[:, 0:COLS - 1]).then_inc(checks, 1)
                dve.wait_ge(checks, done + 2)
                nc.vector.memset(y[:, 2 * CS - 1, 0:COLS:SEGS], 0.0).then_inc(start_ready, 1)
                if not ps.warm:
                    nc.vector.tensor_copy(again[:, :], again_f[:, :]).then_inc(again_ready, 1)

            passes(dve, one_pass)


def kernel(**inputs):
    import numpy as np
    import concourse.bacc as bacc
    from concourse.bass_utils import run_bass_kernel_spmd

    x = np.ascontiguousarray(inputs["x"])
    B, H, W, _ = x.shape
    NS = B * H * W // ST
    w_v = np.asarray(inputs["L0_conv_w_v"]).reshape(C, HP, 2, HS).transpose(0, 2, 3, 1).reshape(C, C)
    side = 2 * WS - 1
    rel = np.asarray(inputs["L0_conv_rel_bias"]).T.reshape(NH, side, side)[:, ::-1, ::-1].transpose(0, 2, 1)
    ffn_w, ffn_v = np.asarray(inputs["L0_ffn_W"]), np.asarray(inputs["L0_ffn_V"])
    sel = np.zeros((2 * N, 130), np.float32)
    for i in range(2 * N):
        sel[i, [i % N, 64 + i % N, 128 + i // N]] = 1.0
    arrays = {
        "x": x.reshape(NS, PW, WS, C),
        "w_q": np.asarray(inputs["L0_conv_w_q"]), "w_k": np.asarray(inputs["L0_conv_w_k"]), "w_v": w_v,
        "w_o": np.asarray(inputs["L0_conv_w_o"]), "b_o": np.asarray(inputs["L0_conv_b_o"]), "rel_bias": rel,
        "ffn_w": ffn_w, "ffn_wT": ffn_w.T, "ffn_vT": ffn_v.T,
        "gamma": np.asarray(inputs["L0_ffn_gamma"]).reshape(C, 1), "beta": np.asarray(inputs["L0_ffn_beta"]).reshape(C, 1),
        "ident": np.eye(128, dtype=np.float32), "sel": sel,
    }
    arrays = {f"in_{k}": np.ascontiguousarray(v) for k, v in arrays.items()}
    nc = bacc.Bacc("TRN2", target_bir_lowering=False, num_devices=1)
    args = [nc.dram_tensor(k, v.shape, mybir.dt.from_np(v.dtype), kind="ExternalInput").ap() for k, v in arrays.items()]
    x1_rec = nc.dram_tensor("x1_rec", (NS, PW, WS, REC), F32, kind="Internal").ap()
    out = nc.dram_tensor("out", (NS * ST, C), F32, kind="ExternalOutput").ap()
    build(nc, B, *args, x1_rec, out)
    r = run_bass_kernel_spmd(nc, [arrays], core_ids=[0])
    return r.results[0]["out"].reshape(x.shape)
```

```python
from contextlib import ExitStack

import concourse.bass as bass
from concourse import mybir

F32 = mybir.dt.float32
BF16 = mybir.dt.bfloat16
I32 = mybir.dt.int32
ALU = mybir.AluOpType
ACT = mybir.ActivationFunctionType
AX_X = mybir.AxisListType.X

C = 128
NH, HS = 8, 16
WS = 7
N = WS * WS
NW = 16
PW = WS * NW
ST = NW * N
HP = NH // 2
PAIRS = NW // 2
SIDE = 2 * WS - 1
RUN = (WS - 1) * SIDE + WS
QR = 64 + N
HN = NH * N
REC = C + 2
HALF = ST // 2
CS = 4
NG = 4
WARM = 16
LN1_EPS, LN2_EPS, BN_EPS = 1e-6, 1e-5, 1e-5
SAME = 1e-6

QPART = (0, 0, 1, 1, 0, 2)
KPART = (0, 1, 0, 1, 2, 0)
ROWS = HS * len(QPART)

SHARED = [("xT", 0, 1, 0), ("xT", 1, 1, 0), ("k", 0, 1, 1), ("k", 1, 1, 1), ("q", 0, 1, 2), ("q", 1, 1, 2),
          ("x2T", 0, -2, 3), ("x2T", 1, -2, 3), ("w", 0, -2, 4), ("w", 1, -2, 4), ("o", 0, -1, 5), ("o", 1, -1, 5),
          ("v", 0, 1, 6), ("v", 1, 1, 6)]
SLOTS = PAIRS
SHIFT_LAG, TURN_LAG, OUT_LAG = 1, 4, 5
LN1_SLOTS = [(3, 0), (3, 1), (6, 2), (7, 3)]
LN2_SLOTS = [(5, 0), (6, 1), (0, 2), (1, 3)]
TILES = [(0, 4), (4, 7)]


def at_strip(dram, strip):
    return dram[bass.ds(strip, 1)].rearrange("s p t c -> (s p) t c")


def at_least(eng, semaphore, value):
    if not (isinstance(value, int) and value <= 0):
        eng.wait_ge(semaphore, value)


def build(nc, images, x, w_q, w_k, w_v, w_o, b_o, rel_bias, ffn_w, ffn_wT, ffn_vT, gamma, beta, ident, x1_rec, out):
    NS = x.shape[0]
    with ExitStack() as ctx:
        def sb(name, shape, dt=F32):
            return ctx.enter_context(nc.sbuf_tensor(name, shape, dt))

        def sem(name):
            return ctx.enter_context(nc.semaphore(name))

        identity = sb("identity", [128, 128])
        ident_b = sb("ident_b", [128, 128], BF16)
        wT_f = sb("wT_f", [128, C])
        minus_half = sb("minus_half", [128, WS])
        w_stats = sb("w_stats", [128, 2 * NS, 6])
        consts = sem("consts")
        made = sem("made")
        phase_a(nc, NS, x, w_q, w_k, w_v, w_o, b_o, rel_bias, ffn_wT, ident, x1_rec,
                identity, ident_b, wT_f, minus_half, w_stats, consts, made)
        phase_b(nc, NS, 2 * NS // images, x1_rec, ffn_w, ffn_vT, gamma, beta, out, identity, minus_half, w_stats)


def phase_a(nc, NS, x, w_q, w_k, w_v, w_o, b_o, rel_bias, ffn_wT, ident, x1_rec,
            identity, ident_b, wT_f, minus_half, w_stats, consts, made):
    with ExitStack() as ctx:
        def sb(name, shape, dt=F32):
            return ctx.enter_context(nc.sbuf_tensor(name, shape, dt))

        def sem(name):
            return ctx.enter_context(nc.semaphore(name))

        wq_in = sb("wq_in", [128, C])
        wk_in = sb("wk_in", [128, C])
        wq = sb("wq", [128, C])
        wk = sb("wk", [128, C])
        wv = sb("wv", [128, C])
        wo = sb("wo", [128, C])
        bo = sb("bo", [3, 4, C])
        bo_r = sb("bo_r", [3, 4, C])
        bo_t = sb("bo_t", [3, 4, C])
        bo_hi = sb("bo_hi", [3, 4, C], BF16)
        bo_mid = sb("bo_mid", [3, 4, C], BF16)
        bo_parts = sb("bo_parts", [3, 4, C], BF16)
        ones = sb("ones", [3, PW], BF16)
        bias_runs = sb("bias_runs", [128, NH, WS * SIDE])
        bias = sb("bias", [128, HN])
        xs = [sb(f"xs{i}", [PW, WS, C]) for i in range(2)]
        rec = [sb(f"rec{i}", [PW, WS, REC]) for i in range(2)]
        bn1 = sb("bn1", [PW, WS, 6])
        mv1 = sb("mv1", [PW, WS, 2])
        consts7 = sb("consts7", [PW, 4])
        st_tmp = [sb(f"st_tmp{i}", [PW, 4, WS, 2]) for i in range(2)]
        xn = sb("xn", [PW, WS, C])
        bn2 = sb("bn2", [PW, WS, 6])
        x2n = sb("x2n", [PW, WS, C])
        xT = sb("xT", [C, NW, N])
        split = {what: [sb(f"{what}_part{i}", [C, ST], BF16) for i in range(3)] for what in "qk"}
        rest = {what: sb(f"{what}_rest", [C, ST]) for what in "qk"}
        qs = [sb(f"qs{i}", [ROWS, NH, ST], BF16) for i in range(2)]
        ks = [sb(f"ks{i}", [ROWS, NH, ST], BF16) for i in range(2)]
        vv = sb("vv", [2 * N, PAIRS, C])
        v2 = [sb(f"v2{i}", [2 * N, NW, C]) for i in range(2)]
        oT = sb("oT", [C, N, NW])
        x2T = sb("x2T", [C, ST])
        negmax = [sb(f"negmax{i}", [128, NH]) for i in range(2)]
        nm_hi = [negmax[i][:, :].bitcast(BF16)[:, 1:2 * NH:2] for i in range(2)]
        nm_lo = [sb(f"nm_lo{i}", [128, NH], BF16) for i in range(2)]
        den = [sb(f"den{i}", [128, NH]) for i in range(4)]
        rden = [sb(f"rden{i}", [128, NH]) for i in range(4)]
        p = [sb(f"p{i}", [128, HN]) for i in range(4)]
        pT = [sb(f"pT{i}", [2 * N, HP, 2, N]) for i in range(2)]
        bank = [ctx.enter_context(nc.psum_tensor(f"bank{i}", [128, 512], F32)) for i in range(8)]
        s_bank, pT_bank, o_bank, sh_bank = bank[0:2], bank[2:4], bank[4:6], bank[6:8]

        x_in = [sem("x_in0"), sem("x_in1")]
        xn_ready = sem("xn_ready")
        x_kept = [sem("x_kept0"), sem("x_kept1")]
        part_ready = {(what, i): sem(f"{what}_part{i}_ready") for what in "qk" for i in range(3)}
        rest_ready = {what: sem(f"{what}_rest_ready") for what in "qk"}
        psum = {k: sem(f"{k}_psum") for k in ("xT", "k", "v", "q", "o", "x2T", "w")}
        evac = {k: sem(f"{k}_evac") for k in ("xT", "v", "o", "x2T", "w")}
        stacked = {what: [sem(f"{what}s_in0"), sem(f"{what}s_in1")] for what in "qk"}
        v2_in = [sem("v2_in0"), sem("v2_in1")]
        rec_out = [sem("rec_out0"), sem("rec_out1")]
        s_psum = sem("s_psum")
        max_ready = sem("max_ready")
        lo_ready = sem("lo_ready")
        marked = sem("marked")
        seeded = sem("seeded")
        shifted = sem("shifted")
        exp_ready = sem("exp_ready")
        sum_ready = sem("sum_ready")
        rden_ready = sem("rden_ready")
        p_ready = sem("p_ready")
        pT_psum = sem("pT_psum")
        pT_evac = sem("pT_evac")
        av_psum = sem("av_psum")
        oT_evac = sem("oT_evac")
        st_steps = [sem("st1_steps"), sem("st2_steps")]
        ve_ready = [sem("ve1_ready"), sem("ve2_ready")]
        bn1_ready = sem("bn1_ready")
        bn2_ready = sem("bn2_ready")
        rs1_ready = sem("rs1_ready")
        rs2_ready = sem("rs2_ready")
        x2n_ready = sem("x2n_ready")
        setup = sem("setup")
        bo_steps = sem("bo_steps")

        READER = {"xT": "act", "k": "act", "v": "act", "q": "act", "x2T": "act", "o": "dve", "w": "dve"}
        released = {**evac, **rest_ready}

        def exists(strip):
            return (not isinstance(strip, int)) or 0 <= strip < NS

        def going(s, g):
            return exists(s if g >= 0 else s - 1)

        def wait_bank(eng, s, use):
            u, back = use, s
            while True:
                u -= 2
                if u < 0:
                    u += len(SHARED)
                    back = back - 1
                if isinstance(back, int) and back < -1:
                    return
                what, part, rel, _ = SHARED[u]
                if exists(back + rel):
                    eng.wait_ge(released[what], 2 * (back + rel) + part + 1)
                    return

        def bodies(eng, body):
            for s in (-2, -1, 0, 1):
                body(s // 2, s % 2)
            with eng.Fori(1, NS // 2 - 1) as half:
                body(half, 0)
                body(half, 1)
            for s in (NS - 2, NS - 1, NS, NS + 1):
                body(s // 2, s % 2)

        block = ctx.enter_context(nc.Block())

        @block.sync
        def _(sp):
            for dst, src in ((wq_in, w_q), (wk_in, w_k), (wv, w_v), (wo, w_o), (wT_f, ffn_wT), (identity, ident)):
                sp.dma_start(dst[:, :], src).then_inc(consts, 16)
            sp.dma_start(bo[:, :, :], b_o).then_inc(consts, 16)
            sp.wait_ge(setup, 9)
            for i in range(2):
                for t in range(WS):
                    src = bass.AP(rel_bias.tensor, rel_bias.offset + SIDE * t, [[1, WS], [SIDE ** 2, NH], [1, RUN]])
                    sp.dma_start(bias_runs[64 * i + WS * t:64 * i + WS * t + WS, :, 0:RUN], src).then_inc(consts, 16)

            def body(half, par):
                s = 2 * half + par
                if exists(s + 2):
                    if exists(s):
                        sp.wait_ge(xn_ready, 2 * (s + 1))
                    sp.dma_start(xs[par][:, :, :], at_strip(x, s + 2)).then_inc(x_in[par], 16)
                for i in range(3):
                    if exists(s + 1):
                        for what, turn, use in (("k", KPART, ks), ("q", QPART, qs)):
                            sp.wait_ge(part_ready[what, i], 2 * (s + 2))
                            for c in range(len(turn)):
                                if turn[c] == i:
                                    sp.dma_start(use[1 - par][HS * c:HS * c + HS, :, 0:ST], split[what][i][:, :])\
                                        .then_inc(stacked[what][1 - par], 16)
                    if i == 0 and exists(s - 2):
                        sp.wait_ge(x2n_ready, 2 * (s - 1))
                        sp.dma_start(at_strip(x1_rec, s - 2), rec[par][:, :, :]).then_inc(rec_out[par], 16)
                if exists(s + 1):
                    sp.wait_ge(evac["v"], 2 * (s + 2))
                    for odd in range(2):
                        for i in range(2):
                            dst = v2[1 - par][odd * N:odd * N + N, :, 64 * odd:64 * odd + 64]
                            sp.dma_start(dst.rearrange("p (q i) c -> p q i c", i=2)[:, :, i, :],
                                         vv[i * N:i * N + N, :, 64 * odd:64 * odd + 64]).then_inc(v2_in[1 - par], 16)
                if exists(s):
                    if not (isinstance(s, int) and s < 2):
                        sp.wait_ge(rec_out[par], 16 * nth(half, par, -2))
                    sp.dma_start(rec[par][:, :, 0:C], at_strip(x, s)).then_inc(x_kept[par], 16)

            bodies(sp, body)
            for i in range(2):
                sp.wait_ge(rec_out[i], 16 * (NS // 2))

        @block.gpsimd
        def _(pool):
            nc.gpsimd.memset(bias_runs[:, :, :], 0.0).then_inc(setup, 1)
            nc.gpsimd.memset(minus_half[:, :], -0.5).then_inc(setup, 1)
            nc.gpsimd.memset(consts7[:, 0:1], 0.5).then_inc(setup, 1)
            nc.gpsimd.memset(consts7[:, 1:2], 1.0 / C).then_inc(setup, 1)
            nc.gpsimd.memset(consts7[:, 2:3], LN1_EPS).then_inc(setup, 1)
            nc.gpsimd.memset(consts7[:, 3:4], LN2_EPS).then_inc(setup, 1)
            nc.gpsimd.memset(ones[:, :], 1.0).then_inc(setup, 1)
            nc.gpsimd.memset(v2[0][:, :, :], 0.0).then_inc(setup, 1)
            nc.gpsimd.memset(v2[1][:, :, :], 0.0).then_inc(setup, 1)
            pool.wait_ge(consts, 16 * NCONST)
            pool.wait_ge(setup, 9)

            def statistics(bn, mean, rstd, eps, which, strip, ready):
                step = st_steps[which]
                t0, t1, t2, t3 = (st_tmp[which][:, k] for k in range(4))
                done = 7 * strip
                pair = bn[:, :, :].rearrange("p t (h k) -> p t h k", h=2)
                TT = nc.gpsimd.tensor_tensor
                half = consts7[:, 0:1, None].to_broadcast([PW, WS, 2])
                per = consts7[:, 1:2, None].to_broadcast([PW, WS, 2])
                at_least(pool, step, done)
                TT(t0, pair[:, :, :, 1], half, ALU.mult).then_inc(step, 1)
                TT(t1, pair[:, :, :, 2], per, ALU.mult).then_inc(step, 1)
                pool.wait_ge(step, done + 2)
                TT(mean, t0[:, :, 0], t0[:, :, 1], ALU.add).then_inc(step, 1)
                TT(t2[:, :, 0], t0[:, :, 0], t0[:, :, 1], ALU.subtract).then_inc(step, 1)
                TT(t3[:, :, 0], t1[:, :, 0], t1[:, :, 1], ALU.add).then_inc(step, 1)
                pool.wait_ge(step, done + 4)
                TT(t2[:, :, 1], t2[:, :, 0], t2[:, :, 0], ALU.mult).then_inc(step, 1)
                pool.wait_ge(step, done + 6)
                TT(t3[:, :, 1], t3[:, :, 0], t2[:, :, 1], ALU.add).then_inc(step, 1)
                pool.wait_ge(step, done + 7)
                TT(t1[:, :, 0], t3[:, :, 1], consts7[:, 2 + which:3 + which].to_broadcast([PW, WS]), ALU.add)\
                    .then_inc(ve_ready[which], 1)
                pool.wait_ge(ve_ready[which], strip + 1)
                TT(rstd, t1[:, :, 0], minus_half[0:PW, :], ALU.pow).then_inc(ready, 1)

            def body(half, par):
                s = 2 * half + par
                for slot in range(SLOTS):
                    g = slot - 1
                    if going(s, g):
                        pool.wait_ge(rden_ready, PAIRS * s + g + 1)
                        pv = p[g % 4][:, :].rearrange("p (h m) -> p h m", h=NH)
                        nc.gpsimd.tensor_tensor(pv, pv, rden[g % 4][:, :, None].to_broadcast([128, NH, N]),
                                                ALU.mult).then_inc(p_ready, 1)

                    for what, i, when in (("k", 0, 2), ("k", 1, 2), ("q", 0, 4), ("q", 1, 4)):
                        if slot == when and exists(s + 1):
                            cols = slice(i * ST // 2, (i + 1) * ST // 2)
                            if i == 0 and exists(s):
                                pool.wait_ge(stacked[what][par], 16 * len(QPART) * nth(half, par))
                            pool.wait_ge(part_ready[what, 1], 2 * (s + 1) + i + 1)
                            nc.gpsimd.tensor_tensor(split[what][2][:, cols], rest[what][:, cols], split[what][1][:, cols],
                                                    ALU.subtract).then_inc(part_ready[what, 2], 1)
                    if slot == 6 and exists(s - 1):
                        pool.wait_ge(bn2_ready, 2 * s)
                        statistics(bn2, rec[1 - par][:, :, C], rec[1 - par][:, :, C + 1], LN2_EPS, 1, s - 1, rs2_ready)
                    if slot == 4 and exists(s + 2):
                        pool.wait_ge(bn1_ready, 2 * s + 6)
                        at_least(pool, xn_ready, 2 * s + 4)
                        statistics(bn1, mv1[:, :, 0], mv1[:, :, 1], LN1_EPS, 0, s + 2, rs1_ready)

            bodies(pool, body)

        @block.tensor
        def _(pe):
            pe.wait_ge(consts, 16 * NCONST)
            pe.wait_ge(setup, 9)
            pe.wait_ge(made, 8)
            for i in range(2):
                nc.tensor.matmul(s_bank[i][:, 0:HN], identity[:, :], bias[:, :], start=True, stop=True).then_inc(marked, 1)

            def shared(s, par, use):
                what, part, rel, _ = SHARED[use]
                if not exists(s + rel):
                    return
                strip = s + rel
                dst = sh_bank[use % 2]
                lo, hi = TILES[part]
                wait_bank(pe, s, use)
                if what == "xT":
                    pe.wait_ge(xn_ready, 2 * strip + part + 1)
                    for t in range(lo, hi):
                        mm = nc.tensor.transpose(dst[:, (t - lo) * PW:(t - lo + 1) * PW], xn[:, t, :],
                                                 identity[0:PW, 0:PW])
                elif what in ("q", "k"):
                    if what == "k":
                        pe.wait_ge(evac["xT"], 2 * (strip + 1))
                    w = wq if what == "q" else wk
                    mm = nc.tensor.matmul(dst[:, 0:ST // 2], w[:, :],
                                          xT[:, part * NW // 2:(part + 1) * NW // 2, :], start=True, stop=True)
                elif what == "v":
                    for i in range(4):
                        pr = 4 * part + i
                        mm = nc.tensor.matmul(dst[0:2 * N, i * C:(i + 1) * C], xT[:, 2 * pr:2 * pr + 2, :], wv[:, :],
                                              start=True, stop=True)
                elif what == "o":
                    pe.wait_ge(oT_evac, 2 * (strip + 1))
                    nc.tensor.matmul(dst[0:PW, 0:(hi - lo) * C], ones[:, :], bo_parts[:, 0:hi - lo, :],
                                     start=True, stop=False, skip_group_check=True)
                    for t in range(lo, hi):
                        mm = nc.tensor.matmul(dst[0:PW, (t - lo) * C:(t - lo + 1) * C],
                                              oT[:, t * WS:(t + 1) * WS, :], wo[:, :], start=False, stop=(t == hi - 1),
                                              skip_group_check=True)
                elif what == "x2T":
                    pe.wait_ge(x2n_ready, 2 * strip + part + 1)
                    for t in range(lo, hi):
                        mm = nc.tensor.transpose(dst[:, (t - lo) * PW:(t - lo + 1) * PW], x2n[:, t, :],
                                                 identity[0:PW, 0:PW])
                else:
                    if part == 0:
                        pe.wait_ge(evac["x2T"], 2 * (strip + 1))
                    mm = nc.tensor.matmul(dst[:, 0:ST // 2], wT_f[:, :], x2T[:, part * (ST // 2):(part + 1) * (ST // 2)],
                                          start=True, stop=True)
                mm.then_inc(psum[what], 1)

            def body(half, par):
                s = 2 * half + par
                for slot in range(SLOTS):
                    g = slot
                    if exists(s):
                        if g == 0:
                            pe.wait_ge(stacked["q"][par], 16 * len(QPART) * nth(half, par))
                            pe.wait_ge(stacked["k"][par], 16 * len(KPART) * nth(half, par))
                        pe.wait_ge(seeded, PAIRS * s + g + 1)
                        for h in range(NH):
                            for i in range(2):
                                w = 2 * g + i
                                mm = nc.tensor.matmul(s_bank[g % 2][64 * i:64 * i + N, N * h:N * h + N],
                                                      qs[par][:, h, N * w:N * w + N], ks[par][:, h, N * w:N * w + N],
                                                      start=False, stop=(i == 1 and h == NH - 1), skip_group_check=True,
                                                      tile_position=(0, 64 * i))
                        mm.then_inc(s_psum, 1)
                    g = slot - SHIFT_LAG
                    if going(s, g):
                        pe.wait_ge(lo_ready, PAIRS * s + g + 1)
                        sb_ = s_bank[g % 2][:, 0:HN]
                        for k, part in enumerate((nm_hi[g % 2], nm_lo[g % 2])):
                            mm = nc.tensor.matmul(sb_, ident_b[:, :], part[:, :, None].to_broadcast([128, NH, N]),
                                                  start=False, stop=(k == 1), skip_group_check=True)
                        mm.then_inc(shifted, 1)
                    for use in range(len(SHARED)):
                        if SHARED[use][3] == slot:
                            shared(s, par, use)
                    g = slot - TURN_LAG
                    if going(s, g):
                        pe.wait_ge(p_ready, PAIRS * s + g + 1)
                        at_least(pe, pT_evac, PAIRS * s + g - 1)
                        for j in range(HP):
                            mm = nc.tensor.transpose(pT_bank[g % 2][0:2 * N, 128 * j:128 * j + QR],
                                                     p[g % 4][0:QR, 2 * N * j:2 * N * (j + 1)],
                                                     identity[0:QR, 0:QR])
                        mm.then_inc(pT_psum, 1)
                    g = slot - OUT_LAG
                    if going(s, g):
                        if g == 0:
                            pe.wait_ge(v2_in[par], 16 * 4 * nth(half, par))
                        pe.wait_ge(pT_evac, PAIRS * s + g + 1)
                        if g % 4 == 0:
                            at_least(pe, oT_evac, 2 * s + g // 4 - 1)
                        for i in range(2):
                            col = (2 * (g % 4) + i) * N
                            for j in range(HP):
                                lhs = v2[par if g >= 0 else 1 - par][:, 2 * (g % PAIRS) + i, j:C:HP]
                                mm = nc.tensor.matmul(o_bank[g % PAIRS // 4][32 * j:32 * j + 32, col:col + N], lhs,
                                                      pT[g % 2][:, j, i, :], start=True, stop=True,
                                                      tile_position=(0, 32 * j))
                        mm.then_inc(av_psum, 1)

            bodies(pe, body)

        @block.scalar
        def _(act):
            def read_shared(half, par, use):
                s = 2 * half + par
                what, part, rel, _ = SHARED[use]
                if READER[what] != "act" or not exists(s + rel):
                    return
                strip = s + rel
                src = sh_bank[use % 2]
                lo, hi = TILES[part]
                act.wait_ge(psum[what], 2 * strip + part + 1)
                if what == "xT":
                    if part == 0:
                        at_least(act, psum["v"], 2 * strip)
                    nn = (hi - lo) * WS
                    ins = nc.scalar.activation(xT[:, :, lo * WS:hi * WS],
                                               src[:, 0:nn * NW].rearrange("p (n w) -> p w n", w=NW), ACT.Copy)
                elif what in ("q", "k"):
                    if part == 0 and exists(strip - 1):
                        act.wait_ge(stacked[what][par], 16 * len(QPART) * nth(half, par))
                    nc.scalar.activation(split[what][0][:, part * (ST // 2):(part + 1) * (ST // 2)],
                                         src[:, 0:ST // 2], ACT.Copy).then_inc(part_ready[what, 0], 1)
                    return
                elif what == "v":
                    if part == 0:
                        wait_v2(half, par, strip)
                    ins = nc.scalar.activation(vv[:, 4 * part:4 * part + 4, :],
                                               src[0:2 * N, :].rearrange("p (q c) -> p q c", c=C), ACT.Copy)
                else:
                    if part == 0:
                        at_least(act, psum["w"], 2 * strip)
                    ins = nc.scalar.activation(x2T[:, lo * PW:hi * PW], src[:, 0:(hi - lo) * PW], ACT.Copy)
                ins.then_inc(evac[what], 1)

            def wait_v2(half, par, strip):
                if exists(strip - 1):
                    act.wait_ge(v2_in[par], 16 * 4 * nth(half, par))

            def body(half, par):
                s = 2 * half + par
                for slot in range(SLOTS):
                    g = slot - SHIFT_LAG
                    if going(s, g):
                        act.wait_ge(shifted, PAIRS * s + g + 1)
                        at_least(act, pT_psum, PAIRS * s + g - 3)
                        nc.scalar.activation(p[g % 4][:, :], s_bank[g % 2][:, 0:HN], ACT.Exp).then_inc(exp_ready, 1)
                        act.wait_ge(exp_ready, PAIRS * s + g + 1)
                        nc.scalar.activation(s_bank[g % 2][:, 0:HN], bias[:, :], ACT.Copy).then_inc(seeded, 1)
                    for use in range(len(SHARED)):
                        if SHARED[use][3] == slot:
                            read_shared(half, par, use)
                    for what, i, when in (("k", 0, 2), ("k", 1, 2), ("q", 0, 3), ("q", 1, 3)):
                        if slot == when and exists(s + 1):
                            cols = slice(i * ST // 2, (i + 1) * ST // 2)
                            act.wait_ge(rest_ready[what], 2 * (s + 1) + i + 1)
                            nc.scalar.activation(split[what][1][:, cols], rest[what][:, cols], ACT.Copy)\
                                .then_inc(part_ready[what, 1], 1)
                    g = slot - TURN_LAG
                    if going(s, g):
                        act.wait_ge(pT_psum, PAIRS * s + g + 1)
                        at_least(act, av_psum, PAIRS * s + g - 1)
                        src = pT_bank[g % 2][0:2 * N, :].rearrange("p (j i n) -> p j i n", j=HP, i=2)[:, :, :, 0:N]
                        nc.scalar.activation(pT[g % 2][:, :, :, :], src, ACT.Copy).then_inc(pT_evac, 1)
                    g = slot - OUT_LAG
                    if g % 4 == 3 and going(s, g):
                        act.wait_ge(av_psum, PAIRS * s + g + 1)
                        at_least(act, psum["o"], 2 * s if g >= 0 else 2 * s - 2)
                        b = g % PAIRS // 4
                        nc.scalar.activation(oT[:, :, 8 * b:8 * b + 8],
                                             o_bank[b][:, 0:8 * N].rearrange("p (w n) -> p n w", n=N),
                                             ACT.Copy).then_inc(oT_evac, 1)

            for i in range(2):
                act.wait_ge(marked, i + 1)
                nc.scalar.activation(s_bank[i][:, 0:HN], bias[:, :], ACT.Copy).then_inc(seeded, 1)
            bodies(act, body)

        @block.vector
        def _(dve):
            dve.wait_ge(consts, 16 * NCONST)
            nc.vector.tensor_copy(ident_b[:, :], identity[:, :]).then_inc(made, 1)
            nc.vector.tensor_copy(bias[:, :].rearrange("p (h t r) -> p h t r", h=NH, t=WS),
                                  bias_runs[:, :, :].rearrange("p h (t r) -> p h t r", t=WS)[:, :, ::-1, WS - 1::-1])\
                .then_inc(made, 1)
            nc.vector.tensor_scalar(wq[:, :].rearrange("c (d h) -> c d h", h=NH),
                                    wq_in[:, :].rearrange("c (h d) -> c d h", h=NH),
                                    float(HS) ** -0.5, None, ALU.mult).then_inc(bo_steps, 1)
            dve.wait_ge(bo_steps, 1)
            nc.vector.tensor_copy(wk[:, :].rearrange("c (d h) -> c d h", h=NH),
                                  wk_in[:, :].rearrange("c (h d) -> c d h", h=NH)).then_inc(made, 1)
            nc.vector.tensor_copy(bo_hi[:, :, :], bo[:, :, :]).then_inc(made, 1)
            dve.wait_ge(made, 4)
            nc.vector.tensor_tensor(bo_r[:, :, :], bo[:, :, :], bo_hi[:, :, :], ALU.subtract).then_inc(made, 1)
            dve.wait_ge(made, 5)
            nc.vector.tensor_copy(bo_mid[:, :, :], bo_r[:, :, :]).then_inc(made, 1)
            dve.wait_ge(made, 6)
            nc.vector.tensor_tensor(bo_r[:, :, :], bo_r[:, :, :], bo_mid[:, :, :], ALU.subtract).then_inc(made, 1)
            dve.wait_ge(made, 7)
            nc.vector.tensor_scalar(bo_r[:, :, :], bo_r[:, :, :], identity[0:3, 2:3], None, ALU.mult).then_inc(bo_steps, 1)
            dve.wait_ge(bo_steps, 2)
            nc.vector.tensor_scalar(bo_t[:, :, :], bo_mid[:, :, :], identity[0:3, 1:2], None, ALU.mult).then_inc(bo_steps, 1)
            dve.wait_ge(bo_steps, 3)
            nc.vector.tensor_tensor(bo_r[:, :, :], bo_r[:, :, :], bo_t[:, :, :], ALU.add).then_inc(bo_steps, 1)
            dve.wait_ge(bo_steps, 4)
            nc.vector.tensor_scalar(bo_t[:, :, :], bo_hi[:, :, :], identity[0:3, 0:1], None, ALU.mult).then_inc(bo_steps, 1)
            dve.wait_ge(bo_steps, 5)
            nc.vector.tensor_tensor(bo_parts[:, :, :], bo_r[:, :, :], bo_t[:, :, :], ALU.add).then_inc(made, 1)

            def ln1(half, par, step):
                s = 2 * half + par
                if not exists(s + 2):
                    return
                if step == 0:
                    dve.wait_ge(x_in[par], 16 * nth(half, par, 2))
                    at_least(dve, rs1_ready, s + 2)
                if step < 2:
                    for t in range(*TILES[step]):
                        ins = nc.vector.bn_stats(bn1[:, t, :], xs[par][:, t, :])
                    ins.then_inc(bn1_ready, 1)
                if step == 2:
                    dve.wait_ge(rs1_ready, s + 3)
                    at_least(dve, psum["xT"], 2 * (s + 2))
                if step >= 2:
                    for t in range(*TILES[step - 2]):
                        ins = nc.vector.tensor_scalar(xn[:, t, :], xs[par][:, t, :], mv1[:, t, 0:1], mv1[:, t, 1:2],
                                                      ALU.subtract, ALU.mult)
                    ins.then_inc(xn_ready, 1)

            def ln2(s, par, step):
                if not exists(s - 1 if step < 2 else s - 2):
                    return
                r = rec[1 - par if step < 2 else par]
                if step == 0:
                    at_least(dve, rs2_ready, s - 1)
                    dve.wait_ge(evac["o"], 2 * s)
                if step < 2:
                    for t in range(*TILES[step]):
                        ins = nc.vector.bn_stats(bn2[:, t, :], r[:, t, 0:C])
                    ins.then_inc(bn2_ready, 1)
                if step == 2:
                    dve.wait_ge(rs2_ready, s - 1)
                    at_least(dve, psum["x2T"], 2 * (s - 2))
                if step >= 2:
                    for t in range(*TILES[step - 2]):
                        ins = nc.vector.tensor_scalar(x2n[:, t, :], r[:, t, 0:C], r[:, t, C:C + 1],
                                                      r[:, t, C + 1:C + 2], ALU.subtract, ALU.mult)
                    ins.then_inc(x2n_ready, 1)

            def take_rest(s, par, use):
                what, i, rel, _ = SHARED[use]
                if what not in rest or not exists(s + rel):
                    return
                strip = s + rel
                if i == 0:
                    at_least(dve, part_ready[what, 2], 2 * strip)
                dve.wait_ge(part_ready[what, 0], 2 * strip + i + 1)
                cols = slice(i * ST // 2, (i + 1) * ST // 2)
                nc.vector.tensor_tensor(rest[what][:, cols], sh_bank[use % 2][:, 0:ST // 2], split[what][0][:, cols],
                                        ALU.subtract).then_inc(rest_ready[what], 1)

            def read_shared(half, par, use):
                s = 2 * half + par
                what, part, rel, _ = SHARED[use]
                if READER[what] != "dve" or not exists(s + rel):
                    return
                strip = s + rel
                src = sh_bank[use % 2]
                lo, hi = TILES[part]
                dve.wait_ge(psum[what], 2 * strip + part + 1)
                if what == "o":
                    if part == 0:
                        dve.wait_ge(x_kept[1 - par], 16 * nth(half, par, -1))
                    nc.vector.tensor_tensor(rec[1 - par][:, lo:hi, 0:C],
                                            src[0:PW, 0:(hi - lo) * C].rearrange("p (t c) -> p t c", c=C),
                                            rec[1 - par][:, lo:hi, 0:C], ALU.add).then_inc(evac["o"], 1)
                else:
                    nc.vector.bn_stats(w_slot(strip, part), src[:, 0:ST // 2]).then_inc(evac["w"], 1)

            def w_slot(strip, part):
                return w_stats[:, bass.ds(2 * strip + part, 1), :]

            def body(half, par):
                s = 2 * half + par
                for slot in range(SLOTS):
                    g = slot
                    if exists(s):
                        dve.wait_ge(s_psum, PAIRS * s + g + 1)
                        at_least(dve, shifted, PAIRS * s + g - 1)
                        nc.vector.tensor_reduce(negmax[g % 2][:, :], s_bank[g % 2][:, 0:HN].rearrange("p (h m) -> p h m", h=NH),
                                                AX_X, ALU.max, negate=True).then_inc(max_ready, 1)
                    if going(s, g - 1):
                        dve.wait_ge(exp_ready, PAIRS * s + g)
                        at_least(dve, rden_ready, PAIRS * s + g - 4)
                        nc.vector.tensor_reduce(den[(g - 1) % 4][:, :], p[(g - 1) % 4][:, :].rearrange("p (h m) -> p h m", h=NH),
                                                AX_X, ALU.add).then_inc(sum_ready, 1)
                    if exists(s):
                        dve.wait_ge(max_ready, PAIRS * s + g + 1)
                        nc.vector.tensor_tensor(nm_lo[g % 2][:, :], negmax[g % 2][:, :], nm_hi[g % 2],
                                                ALU.subtract).then_inc(lo_ready, 1)
                    if going(s, g - 1):
                        dve.wait_ge(sum_ready, PAIRS * s + g)
                        at_least(dve, p_ready, PAIRS * s + g - 4)
                        nc.vector.reciprocal(rden[(g - 1) % 4][:, :], den[(g - 1) % 4][:, :]).then_inc(rden_ready, 1)
                    for use in range(len(SHARED)):
                        if SHARED[use][3] == slot:
                            take_rest(s, par, use)
                            read_shared(half, par, use)
                    for when, step in LN2_SLOTS:
                        if slot == when:
                            ln2(s, par, step)
                    for when, step in LN1_SLOTS:
                        if slot == when:
                            ln1(half, par, step)

            bodies(dve, body)


NCONST = 7 + 2 * WS


def nth(half, par, ahead=0):
    return half + (par + ahead) // 2 + 1


def phase_b(nc, NS, SEGS, x1_rec, ffn_w, ffn_vT, gamma, beta, out, identity, minus_half, w_stats):
    NG = 2 * NS // 128
    COLS = 128 * NG
    CHUNKS = HALF // CS
    WCH = WARM // CS
    recs = x1_rec.rearrange("s p t c -> (s p t) c").rearrange("(g p u) c -> p g u c", g=NG, u=HALF)
    outs = out.rearrange("(g p u) c -> p g u c", g=NG, u=HALF)
    with ExitStack() as ctx:
        def sb(name, shape, dt=F32):
            return ctx.enter_context(nc.sbuf_tensor(name, shape, dt))

        def sem(name):
            return ctx.enter_context(nc.semaphore(name))

        w = sb("w", [C, C])
        vT = sb("vT", [C, C])
        g_col = sb("g_col", [C, 1])
        b_col = sb("b_col", [C, 1])
        w_mv = sb("w_mv", [C, 2])
        w_ve = sb("w_ve", [C, 1])
        w_rs = sb("w_rs", [C, 1])
        a_col = sb("a_col", [C, 1])
        ma_col = sb("ma_col", [C, 1])
        c_col = sb("c_col", [C, 1])
        w_a = sb("w_a", [C, C])
        w_aT = sb("w_aT", [C, C])
        xr = [sb(f"xr{i}", [128, NG, CS, REC]) for i in range(4)]
        xm = sb("xm", [128, NG, CS, C])
        xmT = [sb(f"xmT{i}", [C, NG, CS * 128]) for i in range(2)]
        y = sb("y", [C, 2 * CS, COLS])
        yo = [sb(f"yo{i}", [128, NG, CS, C]) for i in range(2)]
        ends = sb("ends", [C, COLS])
        diff = sb("diff", [C, COLS])
        dmax = sb("dmax", [C, 1])
        dmax1 = sb("dmax1", [1, 1])
        again_f = sb("again_f", [1, 1])
        again = sb("again", [1, 1], I32)
        bank = [ctx.enter_context(nc.psum_tensor(f"bbank{i}", [128, 512], F32)) for i in range(8)]
        z_bank, xT_bank, yT_bank = bank[0:4], bank[4:6], bank[6:8]

        par_in = sem("par_in")
        prep = sem("prep")
        w_ve_ready = sem("w_ve_ready")
        prep_psum = sem("prep_psum")
        x_in = [sem(f"bx_in{i}") for i in range(4)]
        norm_ready = sem("norm_ready")
        xT_psum = sem("bxT_psum")
        xT_ready = sem("bxT_ready")
        z_psum = sem("z_psum")
        y_ready = sem("y_ready")
        yT_psum = sem("yT_psum")
        yo_ready = sem("yo_ready")
        out_done = [sem("out_done0"), sem("out_done1")]
        start_ready = sem("start_ready")
        dmax_ready = sem("dmax_ready")
        dmax_psum = sem("dmax_psum")
        again_ready = sem("again_ready")
        pass_written = sem("pass_written")
        pass_ended = sem("pass_ended")
        checks = sem("checks")

        class Pass:
            def __init__(self, p):
                self.warm = p is None
                self.p = p
                self.n = WCH if self.warm else CHUNKS
                self.offset = CHUNKS - WCH if self.warm else 0
                self.base = 0 if self.warm else WCH + CHUNKS * p
                self.tail_base = 0 if self.warm else CHUNKS * p

            def loads(self, b, q):
                if self.warm:
                    return 1
                return self.p * ((CHUNKS - b + 3) // 4) + 2 + whole(q, b, 4)

            def stores(self, par, q):
                return self.p * (CHUNKS // 2) + 1 + whole(q, par, 2)

        def whole(q, rest, by):
            return (q - rest) // by if isinstance(q, int) else q4[0] * (4 // by) + (q4[1] + q[1] - rest) // by

        q4 = [None, 0]

        def bodies(eng, ps, body):
            first, last = 4, 4 * ((ps.n - 3) // 4)
            if ps.warm or last - first < 8:
                for q in range(-1, ps.n + 1):
                    body(ps, q, q % 4)
                return
            for q in range(-1, first):
                body(ps, q, q % 4)
            with eng.Fori(first // 4, last // 4) as i:
                for k in range(4):
                    q4[:] = [i, k]
                    body(ps, 4 * i + k, k)
            for q in range(last, ps.n + 1):
                body(ps, q, q % 4)

        def passes(eng, one_pass):
            one_pass(Pass(None))
            one_pass(Pass(0))
            eng.wait_ge(again_ready, 1)
            todo = eng.value_load(again[0:1, 0:1], min_val=0, max_val=1)
            with eng.If(todo != 0):
                with eng.Fori(1, SEGS) as p:
                    still = eng.value_load(again[0:1, 0:1], min_val=0, max_val=1)
                    with eng.If(still != 0):
                        one_pass(Pass(p))
                        eng.wait_ge(again_ready, p + 1)
                        eng.sem_inc(pass_ended, 1)

        def has(ps, q):
            return (not isinstance(q, int)) or 0 <= q < ps.n

        block = ctx.enter_context(nc.Block())

        @block.sync
        def _(sp):
            for dst, src in ((w, ffn_w), (vT, ffn_vT), (g_col, gamma), (b_col, beta)):
                sp.dma_start(dst[:, :], src).then_inc(par_in, 16)

            def body(ps, q, k4):
                if has(ps, q + 2) or (isinstance(q, int) and q == -1):
                    for d in ((1, 2) if isinstance(q, int) and q == -1 else (2,)):
                        b = (k4 + d) % 4
                        behind = 3 if not (isinstance(q, int) and q + d < 4) else q + d
                        if ps.warm or (isinstance(ps.p, int) and isinstance(q, int) and q + d < 4):
                            at_least(sp, norm_ready, NG * (ps.base + q + d - behind))
                        else:
                            sp.wait_ge(yo_ready, NG * (ps.tail_base + q + d - behind))
                        sp.dma_start(xr[b][:, :, :, :],
                                     recs[:, :, bass.ds(CS * (ps.offset + q + d), CS), :]).then_inc(x_in[b], 16)
                if has(ps, q - 1) and not ps.warm:
                    par = (k4 - 1) % 2
                    sp.wait_ge(yo_ready, NG * (ps.tail_base + q))
                    sp.dma_start(outs[:, :, bass.ds(CS * (q - 1), CS), :], yo[par][:, :, :, :]).then_inc(out_done[par], 16)

            def one_pass(ps):
                bodies(sp, ps, body)
                if not ps.warm:
                    for par in range(2):
                        sp.wait_ge(out_done[par], 16 * (ps.p + 1) * (CHUNKS // 2))
                        sp.sem_inc(pass_written, 1)

            passes(sp, one_pass)

        @block.tensor
        def _(pe):
            pe.wait_ge(prep, 6)
            nc.tensor.transpose(xT_bank[0][:, 0:C], w_a[:, :], identity[:, :]).then_inc(prep_psum, 1)
            pe.wait_ge(prep, 7)

            def body(ps, q, k4):
                par = k4 % 2
                for k in range(CS):
                    for g in range(NG):
                        if has(ps, q):
                            cols = slice(128 * g, 128 * g + 128)
                            idx = (CS * (ps.base + q) + k) * NG + g
                            if k == 0:
                                pe.wait_ge(xT_ready, NG * (ps.base + q) + g + 1)
                            if isinstance(q, int) and q == 0 and k == 0 and g == 0:
                                pe.wait_ge(start_ready, 1 if ps.warm else ps.p + 2)
                            at_least(pe, y_ready, idx - NG + 1)
                            nc.tensor.matmul(z_bank[g][:, 0:128], w_aT[:, :], xmT[par][:, g, 128 * k:128 * k + 128],
                                             start=True, stop=False)
                            nc.tensor.matmul(z_bank[g][:, 0:128], vT[:, :], y[:, (par * CS + k - 1) % (2 * CS), cols],
                                             start=False, stop=True).then_inc(z_psum, 1)
                    if k < NG and has(ps, q - 1) and not ps.warm:
                        idx = NG * (ps.tail_base + q - 1) + k
                        use = (NG * (k4 - 1) + k) % 2
                        at_least(pe, yo_ready, idx - 1)
                        at_least(pe, y_ready, CS * NG * (ps.base + q))
                        for i in range(CS):
                            mm = nc.tensor.transpose(yT_bank[use][:, 128 * i:128 * i + 128],
                                                     y[:, (1 - par) * CS + i, 128 * k:128 * k + 128], identity[:, :])
                        mm.then_inc(yT_psum, 1)
                    if k < NG and has(ps, q + 1):
                        idx = NG * (ps.base + q + 1) + k
                        use = (NG * (k4 + 1) + k) % 2
                        pe.wait_ge(norm_ready, idx + 1)
                        at_least(pe, xT_ready, idx - 1)
                        for i in range(CS):
                            mm = nc.tensor.transpose(xT_bank[use][:, 128 * i:128 * i + 128], xm[:, k, i, :],
                                                     identity[:, :])
                        mm.then_inc(xT_psum, 1)

            def one_pass(ps):
                bodies(pe, ps, body)
                if not ps.warm:
                    pe.wait_ge(dmax_ready, ps.p + 1)
                    nc.tensor.transpose(xT_bank[0][0:1, 0:128], dmax[:, :], identity[:, :]).then_inc(dmax_psum, 1)

            passes(pe, one_pass)

        @block.scalar
        def _(act):
            def body(ps, q, k4):
                par = k4 % 2
                if not has(ps, q):
                    return
                for k in range(CS):
                    for g in range(NG):
                        idx = (CS * (ps.base + q) + k) * NG + g
                        act.wait_ge(z_psum, idx + 1)
                        nc.scalar.activation(y[:, par * CS + k, 128 * g:128 * g + 128], z_bank[g][:, 0:128],
                                             ACT.Sigmoid, bias=c_col[:, :]).then_inc(y_ready, 1)

            def one_pass(ps):
                bodies(act, ps, body)

            act.wait_ge(prep, 6)
            passes(act, one_pass)

        @block.gpsimd
        def _(pool):
            pool.wait_ge(prep, 1)
            nc.gpsimd.tensor_scalar(w_ve[:, :], w_mv[:, 1:2], BN_EPS, None, ALU.add).then_inc(w_ve_ready, 1)
            pool.wait_ge(w_ve_ready, 1)
            nc.gpsimd.tensor_tensor(w_rs[:, :], w_ve[:, :], minus_half[:, 0:1], ALU.pow).then_inc(prep, 1)

        @block.vector
        def _(dve):
            nc.vector.bn_aggr(w_mv[:, :], w_stats[:, :, :].rearrange("p a b -> p (a b)")).then_inc(prep, 1)
            nc.vector.memset(y[:, 2 * CS - 1, :], 0.0).then_inc(start_ready, 1)
            dve.wait_ge(prep, 1)
            dve.wait_ge(prep, 2)
            dve.wait_ge(par_in, 16 * 4)
            nc.vector.tensor_tensor(a_col[:, :], w_rs[:, :], g_col[:, :], ALU.mult).then_inc(prep, 1)
            dve.wait_ge(prep, 3)
            nc.vector.tensor_tensor(ma_col[:, :], w_mv[:, 0:1], a_col[:, :], ALU.mult).then_inc(prep, 1)
            dve.wait_ge(prep, 4)
            nc.vector.tensor_tensor(c_col[:, :], b_col[:, :], ma_col[:, :], ALU.subtract).then_inc(prep, 1)
            nc.vector.tensor_scalar(w_a[:, :], w[:, :], a_col[:, :], None, ALU.mult).then_inc(prep, 1)
            dve.wait_ge(prep_psum, 1)
            nc.vector.tensor_copy(w_aT[:, :], xT_bank[0][:, 0:C]).then_inc(prep, 1)
            dve.wait_ge(prep, 7)

            def body(ps, q, k4):
                par = k4 % 2
                for k in range(min(CS, NG)):
                    if has(ps, q + 1):
                        b = (k4 + 1) % 4
                        idx = NG * (ps.base + q + 1) + k
                        if k == 0:
                            dve.wait_ge(x_in[b], 16 * ps.loads(b, q + 1 if isinstance(q, int) else after(1)))
                        at_least(dve, xT_psum, idx + 1 - NG)
                        for i in range(CS):
                            ins = nc.vector.tensor_scalar(xm[:, k, i, :], xr[b][:, k, i, 0:C], xr[b][:, k, i, C:C + 1],
                                                          xr[b][:, k, i, C + 1:C + 2], ALU.subtract, ALU.mult)
                        ins.then_inc(norm_ready, 1)
                    if has(ps, q - 1) and not ps.warm:
                        b, op = (k4 - 1) % 4, (k4 - 1) % 2
                        idx = NG * (ps.tail_base + q - 1) + k
                        use = (NG * (k4 - 1) + k) % 2
                        dve.wait_ge(yT_psum, idx + 1)
                        if k == 0 and not (isinstance(q, int) and q < 3 and isinstance(ps.p, int) and ps.p == 0):
                            stores = ps.stores(op, q - 1 if isinstance(q, int) else after(-1)) - 1
                            dve.wait_ge(out_done[op], 16 * stores)
                        nc.vector.tensor_tensor(yo[op][:, k, :, :],
                                                yT_bank[use][:, :].rearrange("p (i c) -> p i c", c=C),
                                                xr[b][:, k, :, 0:C], ALU.add).then_inc(yo_ready, 1)
                    if has(ps, q + 1):
                        idx = NG * (ps.base + q + 1) + k
                        use = (NG * (k4 + 1) + k) % 2
                        dve.wait_ge(xT_psum, idx + 1)
                        at_least(dve, z_psum, CS * NG * (ps.base + q))
                        nc.vector.tensor_copy(xmT[1 - par][:, k, :], xT_bank[use][:, :]).then_inc(xT_ready, 1)

            def after(d):
                return ("after", d)

            steps = [0]

            def one_pass(ps):
                bodies(dve, ps, body)
                last = y[:, 2 * CS - 1, :]
                dve.wait_ge(y_ready, CS * NG * (ps.base + ps.n))
                dve.wait_ge(z_psum, CS * NG * (ps.base + ps.n))
                if ps.warm:
                    done = 0
                else:
                    done = 2 + 5 * ps.p
                    nc.vector.tensor_tensor(diff[:, :], last, ends[:, :], ALU.subtract).then_inc(checks, 1)
                    dve.wait_ge(checks, done + 1)
                    nc.vector.tensor_reduce(dmax[:, :], diff[:, :], AX_X, ALU.max, apply_absolute_value=True)\
                        .then_inc(dmax_ready, 1)
                    dve.wait_ge(dmax_psum, ps.p + 1)
                    nc.vector.tensor_reduce(dmax1[:, :], xT_bank[0][0:1, 0:128], AX_X, ALU.max).then_inc(checks, 1)
                    dve.wait_ge(checks, done + 2)
                    nc.vector.tensor_scalar(again_f[:, :], dmax1[:, :], SAME, None, ALU.is_gt).then_inc(checks, 1)
                    dve.wait_ge(checks, done + 3)
                    done = done + 3
                nc.vector.tensor_copy(ends[:, :], last).then_inc(checks, 1)
                dve.wait_ge(checks, done + 1)
                nc.vector.tensor_copy(y[:, 2 * CS - 1, 1:COLS], ends[:, 0:COLS - 1]).then_inc(checks, 1)
                dve.wait_ge(checks, done + 2)
                nc.vector.memset(y[:, 2 * CS - 1, 0:COLS:SEGS], 0.0).then_inc(start_ready, 1)
                if not ps.warm:
                    nc.vector.tensor_copy(again[:, :], again_f[:, :]).then_inc(again_ready, 1)

            passes(dve, one_pass)


def kernel(**inputs):
    import numpy as np
    import concourse.bacc as bacc
    from concourse.bass_utils import run_bass_kernel_spmd

    x = np.ascontiguousarray(inputs["x"])
    B, H, W, _ = x.shape
    NS = B * H * W // ST
    w_v = np.asarray(inputs["L0_conv_w_v"]).reshape(C, HP, 2, HS).transpose(0, 2, 3, 1).reshape(C, C)
    rel = np.asarray(inputs["L0_conv_rel_bias"]).T.reshape(NH, SIDE, SIDE).transpose(0, 2, 1)
    ffn_w, ffn_v = np.asarray(inputs["L0_ffn_W"]), np.asarray(inputs["L0_ffn_V"])
    arrays = {
        "x": x.reshape(NS, PW, WS, C),
        "w_q": np.asarray(inputs["L0_conv_w_q"]), "w_k": np.asarray(inputs["L0_conv_w_k"]), "w_v": w_v,
        "w_o": np.asarray(inputs["L0_conv_w_o"]), "b_o": np.broadcast_to(np.asarray(inputs["L0_conv_b_o"]), (3, 4, C)), "rel_bias": rel,
        "ffn_w": ffn_w, "ffn_wT": ffn_w.T, "ffn_vT": ffn_v.T,
        "gamma": np.asarray(inputs["L0_ffn_gamma"]).reshape(C, 1), "beta": np.asarray(inputs["L0_ffn_beta"]).reshape(C, 1),
        "ident": np.eye(128, dtype=np.float32),
    }
    arrays = {f"in_{k}": np.ascontiguousarray(v) for k, v in arrays.items()}
    nc = bacc.Bacc("TRN2", target_bir_lowering=False, num_devices=1)
    args = [nc.dram_tensor(k, v.shape, mybir.dt.from_np(v.dtype), kind="ExternalInput").ap() for k, v in arrays.items()]
    x1_rec = nc.dram_tensor("x1_rec", (NS, PW, WS, REC), F32, kind="Internal").ap()
    out = nc.dram_tensor("out", (NS * ST, C), F32, kind="ExternalOutput").ap()
    build(nc, B, *args, x1_rec, out)
    r = run_bass_kernel_spmd(nc, [arrays], core_ids=[0])
    return r.results[0]["out"].reshape(x.shape)
```
